# Optimizing a Trainium2 kernel written in Bass

```python
import numpy as np
import jax
import jax.numpy as jnp

def _softmax(x, axis=-1):
    return jax.nn.softmax(x, axis=axis)

def _gelu(x):
    return jax.nn.gelu(x, approximate=True)

def _silu(x):
    return jax.nn.silu(x)

def _sigmoid(x):
    return jax.nn.sigmoid(x)

def _layernorm(x, axis=-1, eps=1e-05):
    m = jnp.mean(x, axis=axis, keepdims=True)
    v = jnp.var(x, axis=axis, keepdims=True)
    return (x - m) / jnp.sqrt(v + eps)

def _scatter_add(tgt, idx, src, axis=0):
    return tgt.at[idx].add(src)

def _segment_sum(src, seg, n):
    return jax.ops.segment_sum(src, seg, n)
kernel_name = 'mk_decoder_postln_d1_seqx_r4_9d6765'

def setup_inputs(seed: int=0):
    np.random.seed(seed)
    _w = jnp.asarray

    def _rec_inputs():
        import jax
        import jax.numpy as jnp
        _rk = jax.random.key(seed)
        x = -0.0002928 + 1 * jax.random.normal(jax.random.fold_in(_rk, 1), (16, 256, 256), jnp.float32)
        _lenS = 256 - jax.random.randint(jax.random.fold_in(_rk, 7), (16,), 0, max(1, 256 // 4) + 1, jnp.int32)
        _lenS2 = 256 - jax.random.randint(jax.random.fold_in(_rk, 8), (16,), 0, max(1, 256 // 4) + 1, jnp.int32)
        _ctx_1024P = jax.random.normal(jax.random.fold_in(_rk, 11), (16, 16, 256), jnp.float32)
        _ctx_1024c = jax.random.dirichlet(jax.random.fold_in(_rk, 511), 0.3 * jnp.ones((16,), jnp.float32), (16, 256))
        _ctx_1024t = jnp.einsum('bsk,bkd->bsd', _ctx_1024c, _ctx_1024P)
        _ctx_1024t = _ctx_1024t * jax.lax.rsqrt(jnp.mean(jnp.square(_ctx_1024t)) + 1e-12) * 0.953939
        ctx_1024 = -1.39393e-06 + 0.999914 * (_ctx_1024t + 0.3 * jax.random.normal(jax.random.fold_in(_rk, 611), (16, 256, 256), jnp.float32))
        return (x, ctx_1024)
    x, ctx_1024 = _rec_inputs()

    def _L0_attn_setup():
        import jax, jax.numpy as jnp
        import numpy as np
        B, L, D, E, N, DDELTA, DCONV = (4, 512, 256, 512, 16, 64, 4)
        EPS = 1e-05
        key = jax.random.key(seed)
        ks = jax.random.split(key, 12)

        def rn(k, shape, scale=0.02):
            return (jax.random.normal(k, shape) * scale).astype(jnp.float32)
        return {'resid': jax.random.normal(ks[0], (B, L, D), dtype=jnp.float32), 'norm_w': jnp.ones((D,), jnp.float32), 'skip_w': rn(ks[1], (E, D)), 'in_w': rn(ks[2], (E, D)), 'conv_w': rn(ks[3], (E, 1, DCONV), 0.1), 'conv_b': jnp.zeros((E,), jnp.float32), 'Wd1': rn(ks[4], (DDELTA, E)), 'Wd2_w': rn(ks[5], (E, DDELTA)), 'Wd2_b': rn(ks[6], (E,), 0.01), 'WB': rn(ks[7], (N, E)), 'WC': rn(ks[8], (N, E)), 'A_log': (jax.random.normal(ks[9], (E, N)) * 0.5).astype(jnp.float32), 'W_D': jnp.ones((E,), jnp.float32), 'out_w': rn(ks[10], (D, E))}
    _L0_attn_all = _L0_attn_setup()
    _L0_attn_in = {k: v for k, v in _L0_attn_all.items() if k in ('norm_w', 'skip_w', 'in_w', 'conv_w', 'conv_b', 'Wd1', 'Wd2_w', 'Wd2_b', 'WB', 'WC', 'A_log', 'W_D', 'out_w')}
    del _L0_attn_all

    def _L0_xattn_setup():
        import jax, jax.numpy as jnp
        import numpy as np
        D_MODEL = 256
        NUM_HEADS = 16
        D_K = D_MODEL // NUM_HEADS
        BASE = 10000.0

        def _rope_tables(seq_len, d_model, dtype):
            pos = jnp.arange(1, seq_len + 1, dtype=dtype)[:, None]
            theta = BASE ** (-2.0 * jnp.arange(d_model // 2, dtype=dtype) / d_model)
            m_theta = pos * theta
            return (jnp.cos(m_theta), jnp.sin(m_theta))

        def _rotate_half(x):
            d = x.shape[-1]
            return jnp.concatenate([-x[..., d // 2:], x[..., :d // 2]], axis=-1)

        def _apply_rope(x):
            S, D = (x.shape[1], x.shape[2])
            cos, sin = _rope_tables(S, D, x.dtype)
            cos_ri = jnp.repeat(cos, 2, axis=-1)
            sin_ri = jnp.repeat(sin, 2, axis=-1)
            return jax.lax.stop_gradient(x * cos_ri + _rotate_half(x) * sin_ri)
        key = jax.random.key(seed)
        ks = jax.random.split(key, 11)
        B, S, D = (2, 512, D_MODEL)
        scale = 1.0 / np.sqrt(D)
        return {'q': jax.random.normal(ks[0], (B, S, D), jnp.float32), 'k': jax.random.normal(ks[1], (B, S, D), jnp.float32), 'v': jax.random.normal(ks[2], (B, S, D), jnp.float32), 'Wq_w': jax.random.normal(ks[3], (D, D), jnp.float32) * scale, 'Wq_b': jnp.zeros((D,), jnp.float32), 'Wk_w': jax.random.normal(ks[4], (D, D), jnp.float32) * scale, 'Wk_b': jnp.zeros((D,), jnp.float32), 'Wv_w': jax.random.normal(ks[5], (D, D), jnp.float32) * scale, 'Wv_b': jnp.zeros((D,), jnp.float32), 'Wo_w': jax.random.normal(ks[6], (D, D), jnp.float32) * scale, 'Wo_b': jnp.zeros((D,), jnp.float32)}
    _L0_xattn_all = _L0_xattn_setup()
    _L0_xattn_in = {k: v for k, v in _L0_xattn_all.items() if k in ('Wq_w', 'Wq_b', 'Wk_w', 'Wk_b', 'Wv_w', 'Wv_b', 'Wo_w', 'Wo_b')}
    del _L0_xattn_all

    def _L0_ffn_setup():
        import jax, jax.numpy as jnp
        import numpy as np
        S, B, D = (256, 2, 256)
        E, TOPK = (15, 3)
        F = 256
        FS = 512

        def _uinit(k, shape, out_dim):
            std = out_dim ** (-0.5)
            return jax.random.uniform(k, shape, jnp.float32, -std, std)
        key = jax.random.key(seed)
        ks = jax.random.split(key, 10)
        return {'x': jax.random.normal(ks[0], (S, B, D), jnp.float32), 'gate_w': jax.random.normal(ks[1], (E, D), jnp.float32) * D ** (-0.5), 'fc1_w': _uinit(ks[2], (E, 2 * F, D), 2 * F), 'fc1_b': _uinit(ks[3], (E, 2 * F), 2 * F), 'geglu_mult': jnp.ones((E, F), jnp.float32), 'fc2_w': _uinit(ks[4], (E, D, F), D), 'fc2_b': _uinit(ks[5], (E, D), D), 's_fc1_w': _uinit(ks[6], (2 * FS, D), 2 * FS), 's_fc1_b': _uinit(ks[7], (2 * FS,), 2 * FS), 's_geglu_mult': jnp.ones((FS,), jnp.float32), 's_fc2_w': _uinit(ks[8], (D, FS), D), 's_fc2_b': _uinit(ks[9], (D,), D)}
    _L0_ffn_all = _L0_ffn_setup()
    _L0_ffn_in = {k: v for k, v in _L0_ffn_all.items() if k in ('gate_w', 'fc1_w', 'fc1_b', 'geglu_mult', 'fc2_w', 'fc2_b', 's_fc1_w', 's_fc1_b', 's_geglu_mult', 's_fc2_w', 's_fc2_b')}
    del _L0_ffn_all
    return {'x': x, 'ctx_1024': ctx_1024, 'L0_attn_norm_w': _L0_attn_in['norm_w'], 'L0_attn_skip_w': _L0_attn_in['skip_w'], 'L0_attn_in_w': _L0_attn_in['in_w'], 'L0_attn_conv_w': _L0_attn_in['conv_w'], 'L0_attn_conv_b': _L0_attn_in['conv_b'], 'L0_attn_Wd1': _L0_attn_in['Wd1'], 'L0_attn_Wd2_w': _L0_attn_in['Wd2_w'], 'L0_attn_Wd2_b': _L0_attn_in['Wd2_b'], 'L0_attn_WB': _L0_attn_in['WB'], 'L0_attn_WC': _L0_attn_in['WC'], 'L0_attn_A_log': _L0_attn_in['A_log'], 'L0_attn_W_D': _L0_attn_in['W_D'], 'L0_attn_out_w': _L0_attn_in['out_w'], 'L0_xattn_Wq_w': _L0_xattn_in['Wq_w'], 'L0_xattn_Wq_b': _L0_xattn_in['Wq_b'], 'L0_xattn_Wk_w': _L0_xattn_in['Wk_w'], 'L0_xattn_Wk_b': _L0_xattn_in['Wk_b'], 'L0_xattn_Wv_w': _L0_xattn_in['Wv_w'], 'L0_xattn_Wv_b': _L0_xattn_in['Wv_b'], 'L0_xattn_Wo_w': _L0_xattn_in['Wo_w'], 'L0_xattn_Wo_b': _L0_xattn_in['Wo_b'], 'L0_ffn_gate_w': _L0_ffn_in['gate_w'], 'L0_ffn_fc1_w': _L0_ffn_in['fc1_w'], 'L0_ffn_fc1_b': _L0_ffn_in['fc1_b'], 'L0_ffn_geglu_mult': _L0_ffn_in['geglu_mult'], 'L0_ffn_fc2_w': _L0_ffn_in['fc2_w'], 'L0_ffn_fc2_b': _L0_ffn_in['fc2_b'], 'L0_ffn_s_fc1_w': _L0_ffn_in['s_fc1_w'], 'L0_ffn_s_fc1_b': _L0_ffn_in['s_fc1_b'], 'L0_ffn_s_geglu_mult': _L0_ffn_in['s_geglu_mult'], 'L0_ffn_s_fc2_w': _L0_ffn_in['s_fc2_w'], 'L0_ffn_s_fc2_b': _L0_ffn_in['s_fc2_b']}

def reference(x, ctx_1024, L0_attn_norm_w, L0_attn_skip_w, L0_attn_in_w, L0_attn_conv_w, L0_attn_conv_b, L0_attn_Wd1, L0_attn_Wd2_w, L0_attn_Wd2_b, L0_attn_WB, L0_attn_WC, L0_attn_A_log, L0_attn_W_D, L0_attn_out_w, L0_xattn_Wq_w, L0_xattn_Wq_b, L0_xattn_Wk_w, L0_xattn_Wk_b, L0_xattn_Wv_w, L0_xattn_Wv_b, L0_xattn_Wo_w, L0_xattn_Wo_b, L0_ffn_gate_w, L0_ffn_fc1_w, L0_ffn_fc1_b, L0_ffn_geglu_mult, L0_ffn_fc2_w, L0_ffn_fc2_b, L0_ffn_s_fc1_w, L0_ffn_s_fc1_b, L0_ffn_s_geglu_mult, L0_ffn_s_fc2_w, L0_ffn_s_fc2_b):
    import jax
    import jax.numpy as jnp

    def _L0_attn_ref(resid, norm_w, skip_w, in_w, conv_w, conv_b, Wd1, Wd2_w, Wd2_b, WB, WC, A_log, W_D, out_w):
        import jax, jax.numpy as jnp
        import numpy as np
        B, L, D, E, N, DDELTA, DCONV = (4, 512, 256, 512, 16, 64, 4)
        EPS = 1e-05
        x = resid * jax.lax.rsqrt(jnp.mean(resid * resid, axis=-1, keepdims=True) + EPS) * norm_w
        skip = x @ skip_w.T
        x = x @ in_w.T
        xc = jnp.transpose(x, (0, 2, 1))
        xc = jax.lax.conv_general_dilated(xc, conv_w, window_strides=(1,), padding=[(DCONV - 1, 0)], dimension_numbers=('NCH', 'OIH', 'NCH'), feature_group_count=conv_w.shape[0])
        x = jnp.transpose(xc, (0, 2, 1)) + conv_b
        x = jax.nn.silu(x)
        A = -jnp.exp(A_log)
        delta = jax.nn.softplus(x @ Wd1.T @ Wd2_w.T + Wd2_b)
        Bm = x @ WB.T
        Cm = x @ WC.T

        def step(h, inp):
            x_l, d_l, B_l, C_l = inp
            A_bar = jnp.exp(d_l[:, :, None] * A)
            h = A_bar * h + (d_l * x_l)[:, :, None] * B_l[:, None, :]
            y_l = jnp.einsum('ben,bn->be', h, C_l)
            return (h, y_l)
        h0 = jnp.zeros((resid.shape[0], A.shape[0], A.shape[1]), x.dtype)
        xs = (jnp.swapaxes(x, 0, 1), jnp.swapaxes(delta, 0, 1), jnp.swapaxes(Bm, 0, 1), jnp.swapaxes(Cm, 0, 1))
        _, ys = jax.lax.scan(step, h0, xs)
        y = jnp.swapaxes(ys, 0, 1)
        y = y + x * W_D
        y = y * jax.nn.silu(skip)
        y = y @ out_w.T
        return resid + y

    def _L0_xattn_ref(q, k, v, Wq_w, Wq_b, Wk_w, Wk_b, Wv_w, Wv_b, Wo_w, Wo_b):
        import jax, jax.numpy as jnp
        import numpy as np
        D_MODEL = 256
        NUM_HEADS = 16
        D_K = D_MODEL // NUM_HEADS
        BASE = 10000.0

        def _rope_tables(seq_len, d_model, dtype):
            pos = jnp.arange(1, seq_len + 1, dtype=dtype)[:, None]
            theta = BASE ** (-2.0 * jnp.arange(d_model // 2, dtype=dtype) / d_model)
            m_theta = pos * theta
            return (jnp.cos(m_theta), jnp.sin(m_theta))

        def _rotate_half(x):
            d = x.shape[-1]
            return jnp.concatenate([-x[..., d // 2:], x[..., :d // 2]], axis=-1)

        def _apply_rope(x):
            S, D = (x.shape[1], x.shape[2])
            cos, sin = _rope_tables(S, D, x.dtype)
            cos_ri = jnp.repeat(cos, 2, axis=-1)
            sin_ri = jnp.repeat(sin, 2, axis=-1)
            return jax.lax.stop_gradient(x * cos_ri + _rotate_half(x) * sin_ri)
        B, S, D = q.shape
        q = _apply_rope(q)
        k = _apply_rope(k)

        def split_heads(x):
            return x.reshape(B, S, NUM_HEADS, D_K).transpose(0, 2, 1, 3)
        Q = split_heads(q @ Wq_w.T + Wq_b)
        K = split_heads(k @ Wk_w.T + Wk_b)
        V = split_heads(v @ Wv_w.T + Wv_b)
        scores = jnp.einsum('bhqd,bhkd->bhqk', Q, K) / jnp.sqrt(jnp.float32(D_K))
        attn = jax.nn.softmax(scores, axis=-1)
        out = jnp.einsum('bhqk,bhkd->bhqd', attn, V)
        out = out.transpose(0, 2, 1, 3).reshape(B, S, D)
        return out @ Wo_w.T + Wo_b

    def _L0_ffn_ref(x, gate_w, fc1_w, fc1_b, geglu_mult, fc2_w, fc2_b, s_fc1_w, s_fc1_b, s_geglu_mult, s_fc2_w, s_fc2_b):
        import jax, jax.numpy as jnp
        import numpy as np
        S, B, D = (256, 2, 256)
        E, TOPK = (15, 3)
        F = 256
        FS = 512

        def _uinit(k, shape, out_dim):
            std = out_dim ** (-0.5)
            return jax.random.uniform(k, shape, jnp.float32, -std, std)
        s, b, d = x.shape
        xt = x.reshape(-1, d)
        T = xt.shape[0]
        logits = xt @ gate_w.T
        scores = jax.nn.softmax(logits, axis=-1)
        topk_w, topk_idx = jax.lax.top_k(scores, TOPK)
        topk_w = topk_w / (jnp.sum(topk_w, axis=-1, keepdims=True) + 1e-20)
        comb = jnp.zeros((T, E), xt.dtype).at[jnp.arange(T)[:, None], topk_idx].add(topk_w)
        h = jnp.einsum('td,efd->etf', xt, fc1_w) + fc1_b[:, None, :]
        xh, g = (h[..., :F], h[..., F:])
        a = jax.nn.gelu(g, approximate=False) * xh * geglu_mult[:, None, :]
        yexp = jnp.einsum('etf,edf->etd', a, fc2_w) + fc2_b[:, None, :]
        y = jnp.einsum('etd,te->td', yexp, comb)
        hs = xt @ s_fc1_w.T + s_fc1_b
        xs, gs = (hs[..., :FS], hs[..., FS:])
        as_ = jax.nn.gelu(gs, approximate=False) * xs * s_geglu_mult
        ys = as_ @ s_fc2_w.T + s_fc2_b
        return (y + ys).reshape(s, b, d)
    x = _layernorm(x + _L0_attn_ref(x, L0_attn_norm_w, L0_attn_skip_w, L0_attn_in_w, L0_attn_conv_w, L0_attn_conv_b, L0_attn_Wd1, L0_attn_Wd2_w, L0_attn_Wd2_b, L0_attn_WB, L0_attn_WC, L0_attn_A_log, L0_attn_W_D, L0_attn_out_w), axis=-1)
    x = _layernorm(x + _L0_xattn_ref(x, ctx_1024, ctx_1024, L0_xattn_Wq_w, L0_xattn_Wq_b, L0_xattn_Wk_w, L0_xattn_Wk_b, L0_xattn_Wv_w, L0_xattn_Wv_b, L0_xattn_Wo_w, L0_xattn_Wo_b), axis=-1)
    x = _layernorm(x + _L0_ffn_ref(x, L0_ffn_gate_w, L0_ffn_fc1_w, L0_ffn_fc1_b, L0_ffn_geglu_mult, L0_ffn_fc2_w, L0_ffn_fc2_b, L0_ffn_s_fc1_w, L0_ffn_s_fc1_b, L0_ffn_s_geglu_mult, L0_ffn_s_fc2_w, L0_ffn_s_fc2_b), axis=-1)
    return x

_drawn_inputs = setup_inputs


def setup_inputs(seed=0):
    import zlib

    import numpy as np

    out = dict(_drawn_inputs(seed))
    spreads = {'L0_attn_norm_w': (1.0, 0.6),
     'L0_attn_conv_b': (0.0, 0.8),
     'L0_attn_W_D': (1.0, 0.6),
     'L0_xattn_Wq_b': (0.0, 0.445),
     'L0_xattn_Wk_b': (0.0, 2.0),
     'L0_xattn_Wv_b': (0.0, 0.1),
     'L0_xattn_Wo_b': (0.0, 0.1),
     'L0_ffn_geglu_mult': (1.0, 0.6),
     'L0_ffn_s_geglu_mult': (1.0, 0.6)}
    factors = {'L0_attn_skip_w': 8.0,
     'L0_attn_in_w': 8.0,
     'L0_attn_conv_w': 8.0,
     'L0_attn_Wd1': 8.0,
     'L0_attn_Wd2_w': 8.0,
     'L0_attn_Wd2_b': 64.0,
     'L0_attn_WB': 8.0,
     'L0_attn_WC': 8.0,
     'L0_attn_A_log': 8.0,
     'L0_attn_out_w': 8.0,
     'L0_ffn_fc1_b': 8.0,
     'L0_ffn_s_fc1_b': 8.0}
    for name, (base, spread) in spreads.items():
        noise = np.random.default_rng([zlib.crc32(name.encode()), seed]).standard_normal(out[name].shape)
        drawn = base * np.exp(spread * noise) if base else spread * noise
        out[name] = jnp.asarray(drawn.astype(out[name].dtype))
    for name, factor in factors.items():
        out[name] = (out[name] * factor).astype(out[name].dtype)
    return out
```

```python
import numpy as np
import concourse.bass as bass
from concourse import mybir
from contextlib import ExitStack

F32 = mybir.dt.float32
BF16 = mybir.dt.bfloat16
ALU = mybir.AluOpType
ACT = mybir.ActivationFunctionType
AXX = mybir.AxisListType.X

P = 128
B, L, D = 16, 256, 256
T = B * L
TT = L // P
NT = T // P
DC = D // P
EI = 512
EC = EI // P
NS = 16
DD = 64
TAPS = 4
NBC = 2 * NS
RING = 4
LEAD = RING - 1
PARTS = 3
EPS = 1e-5
NE, TOPK, FE, FS = 15, 3, 256, 512
SLOT_TILES = (T * TOPK // P + NE + 1) // 2 * 2
NH = 16
DK = D // NH
HG = 4
SCALE = DK ** -0.5
EXP_LN = "natural_log_exp_and_others"


class Chain:

    def __init__(self, eng, sem, base, per):
        self.eng, self.sem, self.base, self.per, self.n = eng, sem, base, per, 0

    def link(self, ins):
        self.n += 1
        ins.then_inc(self.sem, 1)
        self.eng.wait_ge(self.sem, self.base + self.n)

    def close(self):
        assert self.n == self.per, (self.n, self.per)


def mamba_phase(nc, dram, X, spare, ident):
    with ExitStack() as ctx:
        def sb(name, shape, dt=F32):
            return ctx.enter_context(nc.sbuf_tensor(name, shape, dt))

        def ps(name, shape, dt=F32):
            return ctx.enter_context(nc.psum_tensor(name, shape, dt))

        def sem(name):
            return ctx.enter_context(nc.semaphore(name))

        w_in = sb("w_in", [P, DC, EI])
        w_skip = sb("w_skip", [P, DC, EI])
        w_dbc = sb("w_dbc", [P, EC, DD + PARTS * NBC])
        pick_f = sb("pick_f", [PARTS * NBC, NBC])
        pick = sb("pick", [PARTS * NBC, NBC], BF16)
        w_d2 = sb("w_d2", [DD, EI])
        w_out = sb("w_out", [P, EC, D])
        norm_w = sb("norm_w", [P, DC])
        conv_w = sb("conv_w", [P, EC, TAPS])
        conv_b = sb("conv_b", [P, EC])
        d2_b = sb("d2_b", [P, EC])
        w_D = sb("w_D", [P, EC])
        a_log = sb("a_log", [P, EC, NS])
        a_neg = sb("a_neg", [P, EC, NS])
        conv_diag = sb("conv_diag", [P, EC, TAPS, P])
        d_diag = sb("d_diag", [P, EC, P])
        sq_junk = sb("sq_junk", [P, D])
        ssq = sb("ssq", [P, NT])
        ms = sb("ms", [P, NT])
        rstd = sb("rstd", [P, NT])
        nt1 = sb("nt1", [P, NT])
        nt2 = sb("nt2", [P, NT])
        xn = sb("xn", [P, TT, D])
        xnT = sb("xnT", [P, DC, L])
        xin = sb("xin", [P, EC, TAPS - 1 + L])
        skip_raw = sb("skip_raw", [P, EC, L])
        u = [sb(f"u{j}", [P, EC, L]) for j in range(2)]
        skip = [sb(f"skip{j}", [P, EC, L]) for j in range(2)]
        dlow = sb("dlow", [DD, L])
        bc = sb("bc", [PARTS * NBC, L])
        bc_rest = sb("bc_rest", [PARTS * NBC, L])
        bc_mid = sb("bc_mid", [PARTS * NBC, L], BF16)
        bc_parts = [sb(f"bc_parts{j}", [PARTS * NBC, L], BF16) for j in range(2)]
        delta = [sb(f"delta{j}", [P, EC, L]) for j in range(2)]
        dx = [sb(f"dx{j}", [P, EC, L]) for j in range(2)]
        z = sb("z", [P, EC, L])
        zmiss = sb("zmiss", [P, EC, L])
        zabs = sb("zabs", [P, EC, L])
        zexp = sb("zexp", [P, EC, L])
        zln = sb("zln", [P, EC, L])
        zcor = sb("zcor", [P, EC, L])
        bc_all = sb("bc_all", [P, RING, 2, L])
        rings = spare[:, :, :].rearrange("p t d -> p (t d)").rearrange("p (a r c t) -> p a r c t", a=2, c=EC, t=L)
        decay, inject = rings[:, 0], rings[:, 1]
        h = sb("h", [P, 2, EC, L])
        hc = sb("hc", [P, 2, EC, L])
        y_gated = sb("y_gated", [P, EC, L])
        res = sb("res", [P, TT, D])
        stats = sb("stats", [P, TT, 6])
        mv = sb("mv", [P, TT, 2])
        var = sb("var", [P, TT])
        ln_var = sb("ln_var", [P, TT])
        r0 = sb("r0", [P, TT])
        r1 = sb("r1", [P, TT])
        r2 = sb("r2", [P, TT])

        ps_tr = ps("ps_tr", [P, DC, L])
        ps_pr = ps("ps_pr", [P, EC, L])
        ps_misc = ps("ps_misc", [P, TT * D])
        ps_bc = [ps(f"ps_bc{j}", [P, 2, L]) for j in range(2)]
        ps_y = ps("ps_y", [P, EC, L])

        x_in, w_loaded = sem("x_in"), sem("w_loaded")
        diag_made, rstd_made, ssq_made, ms_made, root_made, exp_a = (
            sem(n) for n in ("diag_made", "rstd_made", "ssq_made", "ms_made", "root_made", "exp_a"))
        pads_zero = sem("pads_zero")
        init_chain = sem("init_chain")
        a_made = sem("a_made")
        f_xn, f_tr, f_xnT, f_in, f_xin, f_skip, f_skip_raw, f_conv, f_u = (
            sem("f_" + n) for n in ("xn", "tr", "xnT", "in", "xin", "skip", "skip_raw", "conv", "u"))
        f_dbc, f_dbc_sb, f_z, f_zsb, f_miss, f_zabs, f_zexp, f_zln, f_cor, f_delta, f_dx, f_bc, f_split = (
            sem("f_" + n) for n in
            ("dbc", "dbc_sb", "z", "zsb", "miss", "zabs", "zexp", "zln", "cor", "delta", "dx", "bc", "split"))
        z_chain = sem("z_chain")
        s_bc, s_bc_all, s_decay, s_inject, s_h, s_hc, s_sum = (
            sem("s_" + n) for n in ("bc", "bc_all", "decay", "inject", "h", "hc", "sum"))
        y_done, y_gated_done, out_done, res_free, ln_var_made, r0_made, var_made, x_made = (
            sem(n) for n in ("y_done", "y_gated_done", "out_done", "res_free", "ln_var_made", "r0_made",
                             "var_made", "x_made"))
        d_chain, s_chain, settled = sem("d_chain"), sem("s_chain"), sem("settled")

        def made(k):
            return k + 1 + RING

        def free(k, ring=RING):
            return k + 1 + RING - ring

        block = ctx.enter_context(nc.Block())

        def steps(eng, body):
            body(0, 0, True, True, False)
            with eng.Fori(0, B // 2 - 2) as i:
                body(i * 2 + 1, 1, True, True, True)
                body(i * 2 + 2, 0, True, True, True)
            body(B - 3, 1, True, True, True)
            body(B - 2, 0, False, True, True)
            body(B - 1, 1, False, False, True)

        def ahead(state, b, q, n, more):
            if n + LEAD < NS:
                state(b, q, n + LEAD)
            elif more:
                state(b + 1, 1 - q, n + LEAD - NS)

        @block.sync
        def _(sp):
            x_t = dram["x"].rearrange("b (s p) d -> p (b s) d", p=P)
            for q in range(4):
                sp.dma_start(X[:, q * NT // 4:(q + 1) * NT // 4, :],
                             x_t[:, q * NT // 4:(q + 1) * NT // 4, :]).then_inc(x_in, 16)

        @block.gpsimd
        def _(g):
            nc.gpsimd.memset(xin[:, :, 0:TAPS - 1], 0.0).then_inc(pads_zero, 1)
            nc.gpsimd.memset(decay[:, :, :, 0:1], 0.0).then_inc(pads_zero, 1)
            g.sem_inc(s_inject, RING)

            def front(b, q):
                g.wait_ge(f_cor, b + 1)
                nc.gpsimd.tensor_tensor(zmiss[:, :, :], zexp[:, :, :], zcor[:, :, :],
                                        ALU.subtract).then_inc(f_miss, 1)

            def state(b, q, n):
                k = b * NS + n
                if n == 0:
                    g.wait_ge(f_dx, b + 1)
                g.wait_ge(s_bc_all, made(k))
                g.wait_ge(s_h, free(k))
                nc.gpsimd.tensor_tensor(
                    inject[:, n % RING, :, :], dx[q][:, :, :],
                    bc_all[:, n % RING, 0, :].unsqueeze(1).to_broadcast([P, EC, L]),
                    ALU.mult).then_inc(s_inject, 1)

            def scan(b, q, with_entry, with_front, with_tail):
                for n in range(NS):
                    ahead(state, b, q, n, with_front)
                    if with_front and n == 11:
                        front(b + 1, 1 - q)

            front(0, 0)
            for n in range(LEAD):
                state(0, 0, n)
            steps(g, scan)

        @block.scalar
        def _(act):
            loads = ((norm_w[:, :], dram["norm_w"]),
                     (w_in[:, :, :], dram["in_wT"].rearrange("(c p) e -> p c e", p=P)),
                     (w_skip[:, :, :], dram["skip_wT"].rearrange("(c p) e -> p c e", p=P)),
                     (conv_w[:, :, :], dram["conv_w"]),
                     (conv_b[:, :], dram["conv_b"]),
                     (w_D[:, :], dram["W_D"]),
                     (w_dbc[:, :, :], dram["dbc_wT"].rearrange("(c p) r -> p c r", p=P)),
                     (w_d2[:, :], dram["Wd2T"]),
                     (d2_b[:, :], dram["Wd2_b"]),
                     (a_log[:, :, :], dram["A_log"]),
                     (pick_f[:, :], dram["pick"]),
                     (w_out[:, :, :], dram["out_wT"].rearrange("(c p) d -> p c d", p=P)))
            for dst, src in loads:
                act.dma_start(dst, src).then_inc(w_loaded, 16)
            act.sem_inc(s_bc_all, RING)
            act.sem_inc(s_decay, RING)
            for t in range(NT):
                if t % (NT // 4) == 0:
                    act.wait_ge(x_in, 16 * 4)
                nc.scalar.activation(sq_junk[:, :], X[:, t, :], ACT.Square,
                                     accum_out=ssq[:, t:t + 1]).then_inc(ssq_made, 1)
                act.wait_ge(ssq_made, t + 1)
            act.wait_ge(ms_made, 1)
            nc.scalar.activation(nt1[:, :], ms[:, :], ACT.Sqrt).then_inc(root_made, 1)
            act.preload_act_table_set(EXP_LN)
            act.wait_ge(w_loaded, 16 * len(loads))
            nc.scalar.activation(a_neg[:, :, :], a_log[:, :, :], ACT.Exp).then_inc(exp_a, 1)

            def norm_x(b):
                for s in range(TT):
                    t = b * TT + s
                    last = nc.scalar.activation(xn[:, s, :], X[:, bass.ds(t, 1), :], ACT.Copy,
                                                scale=rstd[:, bass.ds(t, 1)])
                last.then_inc(f_xn, 1)

            def scale_xT(b):
                act.wait_ge(f_tr, b + 1)
                for c in range(DC):
                    last = nc.scalar.activation(xnT[:, c, :], ps_tr[:, c, :], ACT.Copy,
                                                scale=norm_w[:, c:c + 1])
                last.then_inc(f_xnT, 1)

            def take_xin(b, banks=(0, 2)):
                for c in banks:
                    act.wait_ge(f_in, b * 2 + c // 2 + 1)
                    nc.scalar.activation(xin[:, c:c + 2, TAPS - 1:], ps_pr[:, c:c + 2, :],
                                         ACT.Copy).then_inc(f_xin, 1)

            def take_skip(b, banks=(0, 2)):
                for c in banks:
                    act.wait_ge(f_skip, b * 2 + c // 2 + 1)
                    nc.scalar.activation(skip_raw[:, c:c + 2, :], ps_pr[:, c:c + 2, :],
                                         ACT.Copy).then_inc(f_skip_raw, 1)

            def silus(b, q):
                act.preload_act_table_set("silu_and_others")
                act.wait_ge(f_skip_raw, b * 2 + 2)
                for c in range(EC):
                    if c % 2 == 0:
                        act.wait_ge(f_conv, b * 2 + c // 2 + 1)
                    nc.scalar.activation(u[q][:, c, :], ps_pr[:, c, :], ACT.Silu,
                                         bias=conv_b[:, c:c + 1]).then_inc(f_u, 1)
                nc.scalar.activation(skip[q][:, :, :], skip_raw[:, :, :], ACT.Silu).then_inc(f_u, 1)
                act.preload_act_table_set(EXP_LN)

            def take_dbc(b, q):
                act.wait_ge(f_dbc, b + 1)
                nc.scalar.activation(bc[:, :], ps_misc[0:PARTS * NBC, L:], ACT.Copy).then_inc(f_bc, 1)
                nc.scalar.activation(dlow[:, :], ps_misc[0:DD, 0:L], ACT.Copy).then_inc(f_dbc_sb, 1)

            def softplus(b):
                act.wait_ge(f_zsb, b + 1)
                nc.scalar.activation(zabs[:, :, :], z[:, :, :], ACT.Abs).then_inc(f_zabs, 1)
                act.wait_ge(f_zabs, b + 1)
                nc.scalar.activation(zexp[:, :, :], zabs[:, :, :], ACT.Exp, scale=-1.0).then_inc(f_zexp, 1)
                act.wait_ge(f_zexp, b + 1)
                nc.scalar.activation(zln[:, :, :], zexp[:, :, :], ACT.Ln, bias=1.0).then_inc(f_zln, 1)

            def layernorm_root(b):
                act.wait_ge(var_made, b + 1)
                nc.scalar.activation(ln_var[:, :], var[:, :], ACT.Ln).then_inc(ln_var_made, 1)
                act.wait_ge(ln_var_made, b + 1)
                nc.scalar.activation(r0[:, :], ln_var[:, :], ACT.Exp, scale=-0.5).then_inc(r0_made, 1)

            def state(b, q, n):
                k = b * NS + n
                act.wait_ge(s_bc, k + 1)
                act.wait_ge(s_inject, free(k))
                act.wait_ge(s_hc, free(k))
                nc.scalar.activation(bc_all[:, n % RING, :, :], ps_bc[n % 2][:, :, :],
                                     ACT.Copy).then_inc(s_bc_all, 1)
                if n == 0:
                    act.wait_ge(f_delta, b + 1)
                act.wait_ge(s_h, free(k))
                for c in range(EC):
                    last = nc.scalar.activation(decay[:, n % RING, c, 1:], delta[q][:, c, 1:], ACT.Exp,
                                                scale=a_neg[:, c, n:n + 1])
                last.then_inc(s_decay, 1)

            def scan(b, q, with_entry, with_front, with_tail):
                for n in range(NS):
                    ahead(state, b, q, n, with_front)
                    if with_entry and n == 2:
                        norm_x(b + 2)
                    if with_tail and n == 3:
                        layernorm_root(b - 1)
                    if with_entry and n == 4:
                        scale_xT(b + 2)
                    if with_front and n == 5:
                        silus(b + 1, 1 - q)
                    if with_entry and n == 7:
                        take_xin(b + 2, (0,))
                    if with_front and n == 8:
                        take_dbc(b + 1, 1 - q)
                    if with_entry and n == 8:
                        take_xin(b + 2, (2,))
                    if with_front and n == 10:
                        softplus(b + 1)
                    if with_entry and n == 12:
                        take_skip(b + 2, (0,))
                    if with_entry and n == 13:
                        take_skip(b + 2, (2,))

            act.wait_ge(rstd_made, 1)
            act.wait_ge(a_made, 1)
            norm_x(0)
            scale_xT(0)
            take_xin(0)
            take_skip(0)
            silus(0, 0)
            norm_x(1)
            take_dbc(0, 0)
            scale_xT(1)
            take_xin(1)
            softplus(0)
            for n in range(LEAD):
                state(0, 0, n)
            take_skip(1)
            steps(act, scan)
            layernorm_root(B - 1)

        @block.vector
        def _(v):
            v.sem_inc(s_h, RING)
            v.sem_inc(s_hc, RING)
            v.sem_inc(y_gated_done, 1)
            init = Chain(v, init_chain, 0, 4)
            v.wait_ge(w_loaded, 16 * 12)
            nc.vector.tensor_copy(pick[:, :], pick_f[:, :])
            for c in range(EC):
                for k in range(TAPS):
                    nc.vector.tensor_scalar(conv_diag[:, c, k, :], ident[:, :], conv_w[:, c, k:k + 1], None,
                                            ALU.mult)
                last = nc.vector.tensor_scalar(d_diag[:, c, :], ident[:, :], w_D[:, c:c + 1], None, ALU.mult)
            last.then_inc(diag_made, 1)
            v.wait_ge(ssq_made, NT)
            nc.vector.tensor_scalar(ms[:, :], ssq[:, :], 1.0 / D, EPS, ALU.mult, ALU.add).then_inc(ms_made, 1)
            v.wait_ge(root_made, 1)
            init.link(nc.vector.reciprocal(nt2[:, :], nt1[:, :]))
            init.link(nc.vector.tensor_tensor(nt1[:, :], nt2[:, :], nt2[:, :], ALU.mult))
            init.link(nc.vector.tensor_tensor(nt1[:, :], nt1[:, :], ms[:, :], ALU.mult))
            init.link(nc.vector.tensor_scalar(nt1[:, :], nt1[:, :], -0.5, 1.5, ALU.mult, ALU.add))
            init.close()
            nc.vector.tensor_tensor(rstd[:, :], nt1[:, :], nt2[:, :], ALU.mult).then_inc(rstd_made, 1)
            v.wait_ge(exp_a, 1)
            nc.vector.tensor_scalar(a_neg[:, :, :], a_neg[:, :, :], -1.0, None, ALU.mult).then_inc(a_made, 1)

            def take_z(b):
                v.wait_ge(f_z, b + 1)
                for c in range(EC):
                    last = nc.vector.tensor_scalar(z[:, c, :], ps_pr[:, c, :], d2_b[:, c:c + 1], None, ALU.add)
                last.then_inc(f_zsb, 1)

            def split_bc(b, q):
                v.wait_ge(f_bc, b + 1)
                chain = Chain(v, s_chain, b * 4, 4)
                chain.link(nc.vector.tensor_copy(bc_parts[q][:, :], bc[:, :]))
                chain.link(nc.vector.tensor_tensor(bc_rest[:, :], bc[:, :], bc_parts[q][:, :], ALU.subtract))
                mid, low = slice(NBC, 2 * NBC), slice(2 * NBC, 3 * NBC)
                chain.link(nc.vector.tensor_copy(bc_parts[q][mid, :], bc_rest[mid, :]))
                chain.link(nc.vector.tensor_copy(bc_mid[low, :], bc_rest[low, :]))
                chain.close()
                nc.vector.tensor_tensor(bc_parts[q][low, :], bc_rest[low, :], bc_mid[low, :],
                                        ALU.subtract).then_inc(f_split, 1)

            def one_plus_exp(b):
                v.wait_ge(f_zexp, b + 1)
                nc.vector.tensor_scalar(zcor[:, :, :], zexp[:, :, :], 1.0, -1.0, ALU.add,
                                        ALU.add).then_inc(f_cor, 1)

            def make_delta(b, q):
                v.wait_ge(f_miss, b + 1)
                v.wait_ge(z_chain, b + 1)
                nc.vector.tensor_tensor(delta[q][:, :, :], z[:, :, :], zmiss[:, :, :], ALU.add).then_inc(f_delta, 1)

            def add_log(b):
                v.wait_ge(f_zln, b + 1)
                nc.vector.scalar_tensor_tensor(z[:, :, :], z[:, :, :], 0.0, zln[:, :, :],
                                               ALU.max, ALU.add).then_inc(z_chain, 1)

            def make_dx(b, q):
                v.wait_ge(f_delta, b + 1)
                v.wait_ge(f_u, (b + 1) * (EC + 1))
                nc.vector.tensor_tensor(dx[q][:, :, :], delta[q][:, :, :], u[q][:, :, :],
                                        ALU.mult).then_inc(f_dx, 1)

            def scan(b, q, with_entry, with_front, with_tail):
                for n in range(NS):
                    k = b * NS + n
                    if n == 3 and with_tail:
                        residual(b - 1)
                    if n == 5 and with_tail:
                        normalize(b - 1)
                    v.wait_ge(s_decay, made(k))
                    v.wait_ge(s_inject, made(k))
                    nc.vector.tensor_tensor_scan(
                        h[:, n % 2, :, :].rearrange("p c t -> p (c t)"),
                        decay[:, n % RING, :, :].rearrange("p c t -> p (c t)"),
                        inject[:, n % RING, :, :].rearrange("p c t -> p (c t)"),
                        0.0, ALU.mult, ALU.add).then_inc(s_h, 1)
                    if n == 0 and with_tail:
                        gate(b - 1, 1 - q)
                    v.wait_ge(s_h, made(k))
                    v.wait_ge(s_bc_all, made(k))
                    v.wait_ge(s_sum, free(k, 2))
                    nc.vector.tensor_tensor(
                        hc[:, n % 2, :, :], h[:, n % 2, :, :],
                        bc_all[:, n % RING, 1:2, :].to_broadcast([P, EC, L]), ALU.mult).then_inc(s_hc, 1)
                    if with_front and n == 9:
                        split_bc(b + 1, 1 - q)
                    if with_front and n == 10:
                        take_z(b + 1)
                    if with_front and n == 11:
                        one_plus_exp(b + 1)
                    if with_front and n == 12:
                        add_log(b + 1)
                        make_delta(b + 1, 1 - q)
                    if with_front and n == 13:
                        make_dx(b + 1, 1 - q)

            def gate(b, q):
                v.wait_ge(y_done, b + 1)
                v.sem_inc(s_sum, 1)
                nc.vector.tensor_tensor(y_gated[:, :, :], ps_y[:, :, :], skip[q][:, :, :],
                                        ALU.mult).then_inc(y_gated_done, 1)

            def residual(b):
                v.wait_ge(out_done, b + 1)
                chain = Chain(v, d_chain, b * 6, 3)
                x_b = X[:, bass.ds(b * TT, TT), :]
                chain.link(nc.vector.scalar_tensor_tensor(
                    res[:, :, :], x_b, 2.0, ps_misc[:, :].rearrange("p (s d) -> p s d", s=TT),
                    ALU.mult, ALU.add))
                v.sem_inc(res_free, 1)
                for s in range(TT):
                    last = nc.vector.bn_stats(stats[:, s, :], res[:, s, :])
                chain.link(last)
                v.sem_inc(settled, 1)
                for s in range(TT):
                    last = nc.vector.bn_aggr(mv[:, s, :], stats[:, s, :])
                chain.link(last)
                chain.close()
                nc.vector.tensor_scalar(var[:, :], mv[:, :, 1], EPS, None, ALU.add).then_inc(var_made, 1)

            def normalize(b):
                v.wait_ge(r0_made, b + 1)
                chain = Chain(v, d_chain, b * 6 + 3, 3)
                chain.link(nc.vector.tensor_tensor(r1[:, :], r0[:, :], r0[:, :], ALU.mult))
                chain.link(nc.vector.tensor_tensor(r1[:, :], r1[:, :], var[:, :], ALU.mult))
                chain.link(nc.vector.tensor_scalar(r1[:, :], r1[:, :], -0.5, 1.5, ALU.mult, ALU.add))
                chain.close()
                nc.vector.tensor_tensor(r2[:, :], r1[:, :], r0[:, :], ALU.mult).then_inc(x_made, 1)
                v.wait_ge(x_made, b * 2 + 1)
                for s in range(TT):
                    last = nc.vector.tensor_scalar(X[:, bass.ds(b * TT + s, 1), :], res[:, s, :],
                                                   mv[:, s, 0:1], r2[:, s:s + 1], ALU.subtract, ALU.mult)
                last.then_inc(x_made, 1)

            split_bc(0, 0)
            take_z(0)
            one_plus_exp(0)
            add_log(0)
            make_delta(0, 0)
            make_dx(0, 0)
            steps(v, scan)
            gate(B - 1, 1)
            residual(B - 1)
            normalize(B - 1)
            v.wait_ge(x_made, 2 * B)

        @block.tensor
        def _(pe):
            pe.sem_inc(s_sum, RING)

            def transposes(b):
                pe.wait_ge(f_xn, b + 1)
                for c in range(DC):
                    for s in range(TT):
                        last = nc.tensor.transpose(ps_tr[:, c, s * P:(s + 1) * P],
                                                   xn[:, s, c * P:(c + 1) * P], ident[:, :])
                last.then_inc(f_tr, 1)

            def project(w, chunks, done):
                for c in chunks:
                    for k in range(DC):
                        last = nc.tensor.matmul(ps_pr[:, c, :], w[:, k, c * P:(c + 1) * P], xnT[:, k, :],
                                                start=(k == 0), stop=(k == DC - 1))
                    if c % 2 == 1:
                        last.then_inc(done, 1)

            def project_in(b, chunks):
                if chunks[0] == 0:
                    pe.wait_ge(f_xnT, b + 1)
                for c in chunks:
                    if c % 2 == 0 and not (isinstance(b, int) and b == 0):
                        pe.wait_ge(f_u, (b - 1) * (EC + 1) + c + 2)
                    project(w_in, (c,), f_in)

            def project_skip(b, chunks):
                for c in chunks:
                    if c % 2 == 0:
                        pe.wait_ge(f_xin, b * 2 + c // 2 + 1)
                        if c == 0 and not (isinstance(b, int) and b == 0):
                            pe.wait_ge(f_zsb, b)
                    project(w_skip, (c,), f_skip)

            def conv(b, chunks):
                for c in chunks:
                    if c % 2 == 0:
                        pe.wait_ge(f_skip_raw, b * 2 + c // 2 + 1)
                    for k in range(TAPS):
                        last = nc.tensor.matmul(ps_pr[:, c, :], conv_diag[:, c, k, :], xin[:, c, k:k + L],
                                                start=(k == 0), stop=(k == TAPS - 1))
                    if c % 2 == 1:
                        last.then_inc(f_conv, 1)

            def project_u(b, q, at, n, col):
                for k in range(EC):
                    last = nc.tensor.matmul(ps_misc[0:n, col:col + L], w_dbc[:, k, at:at + n], u[q][:, k, :],
                                            start=(k == 0), stop=(k == EC - 1))
                return last

            def delta_low(b, q):
                pe.wait_ge(f_u, b * (EC + 1) + EC)
                project_u(b, q, 0, DD, 0)

            def rows_b_c(b, q):
                project_u(b, q, DD, PARTS * NBC, L).then_inc(f_dbc, 1)

            def delta_up(b, q, with_entry):
                pe.wait_ge(f_dbc_sb, b + 1)
                if with_entry:
                    pe.wait_ge(f_xin, b * 2 + 4)
                for c in range(EC):
                    last = nc.tensor.matmul(ps_pr[:, c, :], w_d2[:, c * P:(c + 1) * P], dlow[:, :],
                                            start=True, stop=True)
                last.then_inc(f_z, 1)

            def spread(b, q, n):
                if n == 0:
                    pe.wait_ge(f_split, b + 1)
                k = b * NS + n
                pe.wait_ge(s_bc_all, free(k, 2))
                for j in range(2):
                    at = j * NS + n
                    last = nc.tensor.matmul(ps_bc[n % 2][:, j, :],
                                            pick[:, at:at + 1].to_broadcast([PARTS * NBC, P]),
                                            bc_parts[q][:, :], start=True, stop=True)
                last.then_inc(s_bc, 1)

            def add_state(b, n):
                k = b * NS + n
                if n == 0:
                    pe.wait_ge(y_gated_done, b + 1)
                pe.wait_ge(s_hc, made(k))
                for c in range(0, EC, 2):
                    last = nc.tensor.matmul(ps_y[:, c:c + 2, :], ident[:, :], hc[:, n % 2, c:c + 2, :],
                                            start=(n == 0), stop=(n == NS - 1))
                last.then_inc(s_sum if n < NS - 1 else y_done, 1)

            def add_input(b, q):
                for c in range(EC):
                    nc.tensor.matmul(ps_y[:, c, :], d_diag[:, c, :], u[q][:, c, :],
                                     start=False, stop=False, skip_group_check=True)

            def scan(b, q, with_entry, with_front, with_tail):
                for n in range(NS):
                    ahead(spread, b, q, n, with_front)
                    if with_front and n == 0:
                        conv(b + 1, (0,))
                    if with_tail and n in (1, 2):
                        project_out(b - 1, n - 1)
                    if with_entry and n == 3:
                        transposes(b + 2)
                    if with_front and n in (3, 4, 5):
                        conv(b + 1, (n - 2,))
                    if with_entry and n == 6:
                        project_in(b + 2, (0, 1))
                    if with_front and n == 7:
                        if with_tail:
                            pe.wait_ge(res_free, b)
                        delta_low(b + 1, 1 - q)
                    if with_front and n == 8:
                        rows_b_c(b + 1, 1 - q)
                    if with_entry and n == 8:
                        project_in(b + 2, (2, 3))
                    if with_front and n == 9:
                        delta_up(b + 1, 1 - q, with_entry)
                    if with_entry and n == 11:
                        project_skip(b + 2, (0, 1))
                    if with_entry and n == 12:
                        project_skip(b + 2, (2, 3))
                    add_state(b, n)
                    if n == 0:
                        add_input(b, q)

            def project_out(b, s):
                if s == 0:
                    pe.wait_ge(y_gated_done, b + 2)
                for k in range(EC):
                    last = nc.tensor.matmul(ps_misc[:, s * D:(s + 1) * D],
                                            y_gated[:, k, s * P:(s + 1) * P], w_out[:, k, :],
                                            start=(k == 0), stop=(k == EC - 1))
                if s == TT - 1:
                    last.then_inc(out_done, 1)

            pe.wait_ge(w_loaded, 16 * 12)
            pe.wait_ge(diag_made, 1)
            pe.wait_ge(pads_zero, 2)
            transposes(0)
            project_in(0, range(EC))
            project_skip(0, range(EC))
            conv(0, range(EC))
            delta_low(0, 0)
            rows_b_c(0, 0)
            transposes(1)
            project_in(1, range(EC))
            delta_up(0, 0, True)
            for n in range(LEAD):
                spread(0, 0, n)
            project_skip(1, range(EC))
            steps(pe, scan)
            for s in range(TT):
                project_out(B - 1, s)


def attention_phase(nc, dram, X, ident):
    with ExitStack() as ctx:
        def sb(name, shape, dt=F32):
            return ctx.enter_context(nc.sbuf_tensor(name, shape, dt))

        def ps(name, shape, dt=F32):
            return ctx.enter_context(nc.psum_tensor(name, shape, dt))

        def sem(name):
            return ctx.enter_context(nc.semaphore(name))

        wq, wk, wv = (sb(n, [P, DC, D]) for n in ("wq", "wk", "wv"))
        wo = sb("wo", [P, HG, D])
        bq, bk, head_even, head_odd = (sb(n, [P, DC]) for n in ("bq", "bk", "head_even", "head_odd"))
        bv, bo = sb("bv", [P, D]), sb("bo", [P, D])
        cos, sin = sb("cos", [P, DC, L]), sb("sin", [P, DC, L])
        ctxT = [sb(f"ctxT{j}", [P, DC, L]) for j in range(2)]
        xs = sb("xs", [P, TT, D])
        rope_a, rope_b, qr = (sb(n, [P, DC, L]) for n in ("rope_a", "rope_b", "qr"))
        krope_a, krope_b = sb("krope_a", [P, DC, L]), sb("krope_b", [P, DC, L])
        kr = sb("kr", [P, DC, L])
        QT = [sb(f"QT{j}", [P, DC, L]) for j in range(2)]
        KT = [sb(f"KT{j}", [P, 2, DC, L]) for j in range(2)]
        V = [sb(f"V{j}", [P, TT, NH, 32]) for j in range(2)]
        neg_max = sb("neg_max", [P, 2, TT])
        prob = sb("prob", [P, 2, TT, L])
        total = sb("total", [P, 2, TT])
        inv = sb("inv", [P, 2, TT])
        probT = sb("probT", [P, 2 * HG, TT, L])
        oT = sb("oT", [P, HG, L])
        res = sb("a_res", [P, TT, D])
        stats, mv, var = sb("a_stats", [P, TT, 6]), sb("a_mv", [P, TT, 2]), sb("a_var", [P, TT])
        ln_var, r0, r1, r2 = (sb(n, [P, TT]) for n in ("a_ln_var", "a_r0", "a_r1", "a_r2"))

        ps_m0 = ps("ps_m0", [P, 2, 256])
        ps_m1 = ps("ps_m1", [P, 2, 256])
        ps_s = [ps(f"ps_s{j}", [P, TT, L]) for j in range(2)]
        ps_t = [ps(f"ps_t{j}", [P, TT, L]) for j in range(2)]
        ps_o = ps("ps_o", [P, HG, L])

        w_got, v_zero, bq_scaled = sem("w_got"), sem("v_zero"), sem("bq_scaled")
        ctx_in = [sem(f"ctx_in{j}") for j in range(2)]
        f_xs, f_tr, f_qr, f_kr, f_q, f_qs, f_k, f_ks, f_v, f_vs = (
            sem("af_" + n) for n in ("xs", "tr", "qr", "kr", "q", "qs", "k", "ks", "v", "vs"))
        q_chain, k_chain, n_chain = sem("q_chain"), sem("k_chain"), sem("n_chain")
        h_s, h_max, h_exp, h_inv, h_norm, h_t, h_pt, h_pv = (
            sem("h_" + n) for n in ("s", "max", "exp", "inv", "norm", "t", "pt", "pv"))
        t_o, t_w, t_res, t_var, t_lnv, t_r0, t_x, t_settled = (
            sem("t_" + n) for n in ("o", "w", "res", "var", "lnv", "r0", "x", "settled"))
        block = ctx.enter_context(nc.Block())

        def made(k):
            return k + 1 + 2

        def free(k):
            return k + 1

        loads = ((wq[:, :, :], dram["WqT"].rearrange("(c p) e -> p c e", p=P)),
                 (wk[:, :, :], dram["WkT"].rearrange("(c p) e -> p c e", p=P)),
                 (wv[:, :, :], dram["WvT"].rearrange("(c p) e -> p c e", p=P)),
                 (wo[:, :, :], dram["WoT"].rearrange("(c p) e -> p c e", p=P)),
                 (bq[:, :], dram["bq"]), (bk[:, :], dram["bk"]),
                 (head_even[:, :], dram["head_even"]), (head_odd[:, :], dram["head_odd"]),
                 (bv[:, :], dram["bv"].to_broadcast([P, D])), (bo[:, :], dram["bo"].to_broadcast([P, D])),
                 (cos[:, :, :], dram["cosT"].rearrange("(c p) t -> p c t", p=P)),
                 (sin[:, :, :], dram["sinT"].rearrange("(c p) t -> p c t", p=P)))

        def steps(eng, body):
            body(0, 0, True, False)
            with eng.Fori(0, B // 2 - 1) as i:
                body(i * 2 + 1, 1, True, True)
                body(i * 2 + 2, 0, True, True)
            body(B - 1, 1, False, True)

        @block.sync
        def _(sp):
            ctx_v = dram["ctxT"].rearrange("b (c p) t -> p b c t", p=P)

            def load_ctx(b, q, count):
                sp.dma_start(ctxT[q][:, :, :], ctx_v[:, bass.ds(b, 1), :, :]).then_inc(ctx_in[q], 16)

            load_ctx(0, 0, 1)
            for dst, src in loads:
                sp.dma_start(dst, src).then_inc(w_got, 16)
            load_ctx(1, 1, 1)
            with sp.Fori(0, B // 2 - 1) as i:
                for q in range(2):
                    b = i * 2 + q
                    sp.wait_ge(f_v, b + 1)
                    sp.wait_ge(f_kr, b + 1)
                    load_ctx(b + 2, q, i + 2)

        @block.gpsimd
        def _(g):
            for q in range(2):
                nc.gpsimd.memset(V[q][:, :, :, :], 0.0).then_inc(v_zero, 1)

            def front(b, q, loads_before):
                g.wait_ge(ctx_in[q], loads_before * 16 + 16)
                chain = Chain(g, k_chain, b * 2, 2)
                nc.gpsimd.tensor_tensor(krope_a[:, :, :], ctxT[q][:, :, :], cos[:, :, :], ALU.mult)
                for c in range(DC):
                    last = nc.gpsimd.tensor_tensor(krope_b[:, c, :], ctxT[q][:, 1 - c, :], sin[:, c, :],
                                                   ALU.mult)
                chain.link(last)
                if not (isinstance(b, int) and b == 0):
                    g.wait_ge(f_k, b)
                chain.link(nc.gpsimd.tensor_tensor(kr[:, :, :], krope_a[:, :, :], krope_b[:, :, :], ALU.add))
                chain.close()
                g.sem_inc(f_kr, 1)

            g.wait_ge(w_got, 16 * len(loads))
            front(0, 0, 0)
            front(1, 1, 0)
            with g.Fori(0, B // 2 - 1) as i:
                front(i * 2 + 2, 0, i + 1)
                front(i * 2 + 3, 1, i + 1)

        @block.scalar
        def _(act):
            act.sem_inc(h_exp, 2)
            act.sem_inc(h_pt, 2)
            act.preload_act_table_set(EXP_LN)

            def copy_x(b):
                nc.scalar.activation(xs[:, :, :], X[:, bass.ds(b * TT, TT), :], ACT.Copy).then_inc(f_xs, 1)

            def take_q(b, q):
                act.wait_ge(f_q, b + 1)
                for c in range(DC):
                    last = nc.scalar.activation(QT[q][:, c, :], ps_m1[:, c, :], ACT.Identity,
                                                bias=bq[:, c:c + 1], scale=SCALE)
                last.then_inc(f_qs, 1)

            def exps(k, j):
                act.wait_ge(h_max, k + 1)
                act.wait_ge(h_t, free(k))
                for s in range(TT):
                    last = nc.scalar.activation(prob[:, j, s, :], ps_s[j][:, s, :], ACT.Exp,
                                                bias=neg_max[:, j, s:s + 1], accum_out=total[:, j, s:s + 1])
                last.then_inc(h_exp, 1)

            def take_t(k, G, h):
                act.wait_ge(h_t, made(k))
                if h % HG == 0:
                    act.wait_ge(h_pv, free(G))
                nc.scalar.activation(probT[:, h % (2 * HG), :, :], ps_t[h % 2][:, :, :],
                                     ACT.Copy).then_inc(h_pt, 1)

            def heads(b, q, with_front, with_tail):
                for h in range(NH):
                    k = b * NH + h
                    if h < NH - 1 or with_front:
                        exps(k + 1, (h + 1) % 2)
                    take_t(k, b * (NH // HG) + h // HG, h)
                    if with_tail and h == 1:
                        tail_o(b - 1)
                    if with_tail and h == 4:
                        tail_root(b - 1)
                    if with_front and h == 2:
                        copy_x(b + 1)
                    if with_front and h == 7:
                        take_q(b + 1, 1 - q)

            def tail_o(b):
                act.wait_ge(h_pv, made(b * (NH // HG) + NH // HG - 1))
                nc.scalar.activation(oT[:, :, :], ps_o[:, :, :], ACT.Copy).then_inc(t_o, 1)

            def tail_root(b):
                act.wait_ge(t_var, b + 1)
                nc.scalar.activation(ln_var[:, :], var[:, :], ACT.Ln).then_inc(t_lnv, 1)
                act.wait_ge(t_lnv, b + 1)
                nc.scalar.activation(r0[:, :], ln_var[:, :], ACT.Exp, scale=-0.5).then_inc(t_r0, 1)

            act.wait_ge(w_got, 16 * len(loads))
            copy_x(0)
            act.wait_ge(bq_scaled, 1)
            take_q(0, 0)
            exps(0, 0)
            steps(act, heads)
            tail_o(B - 1)
            tail_root(B - 1)

        @block.vector
        def _(v):
            v.wait_ge(w_got, 16 * len(loads))
            nc.vector.tensor_scalar(bq[:, :], bq[:, :], SCALE, None, ALU.mult).then_inc(bq_scaled, 1)

            def rope_q(b):
                v.wait_ge(f_tr, b + 1)
                chain = Chain(v, q_chain, b, 1)
                nc.vector.tensor_tensor(rope_a[:, :, :], ps_m0[:, :, :], cos[:, :, :], ALU.mult)
                for c in range(DC):
                    last = nc.vector.tensor_tensor(rope_b[:, c, :], ps_m0[:, 1 - c, :], sin[:, c, :], ALU.mult)
                chain.link(last)
                nc.vector.tensor_tensor(qr[:, :, :], rope_a[:, :, :], rope_b[:, :, :], ALU.add).then_inc(f_qr, 1)

            def take_k(b, q):
                v.wait_ge(f_k, b + 1)
                for c in range(DC):
                    for odd, mask in enumerate((head_even, head_odd)):
                        last = nc.vector.tensor_scalar(KT[q][:, odd, c, :], ps_m0[:, c, :], bk[:, c:c + 1],
                                                       mask[:, c:c + 1], ALU.add, ALU.mult)
                last.then_inc(f_ks, 1)

            def take_v(b, q):
                v.wait_ge(f_v, b + 1)
                for s in range(TT):
                    last = nc.vector.tensor_tensor(
                        V[q][:, s, :, 0:DK], ps_m1[:, s, :].rearrange("p (h d) -> p h d", h=NH),
                        bv[:, :].rearrange("p (h d) -> p h d", h=NH), ALU.add)
                last.then_inc(f_vs, 1)

            def row_max(k, j):
                v.wait_ge(h_s, k + 1)
                nc.vector.tensor_reduce(neg_max[:, j, :], ps_s[j][:, :, :], AXX, ALU.max,
                                        negate=True).then_inc(h_max, 1)

            def normalize(k, j):
                v.wait_ge(h_exp, made(k))
                nc.vector.reciprocal(inv[:, j, :], total[:, j, :]).then_inc(h_inv, 1)
                v.wait_ge(h_inv, k + 1)
                for s in range(TT):
                    last = nc.vector.tensor_scalar(prob[:, j, s, :], prob[:, j, s, :], inv[:, j, s:s + 1],
                                                   None, ALU.mult)
                last.then_inc(h_norm, 1)

            def tail_res(b):
                v.wait_ge(t_w, b + 1)
                chain = Chain(v, n_chain, b * 6, 3)
                chain.link(nc.vector.tensor_tensor(res[:, :, :], X[:, bass.ds(b * TT, TT), :], ps_m0[:, :, :],
                                                   ALU.add))
                v.sem_inc(t_res, 1)
                chain.link(nc.vector.tensor_tensor(res[:, :, :], res[:, :, :],
                                                   bo[:, :].unsqueeze(1).to_broadcast([P, TT, D]), ALU.add))
                for s in range(TT):
                    last = nc.vector.bn_stats(stats[:, s, :], res[:, s, :])
                chain.link(last)
                v.sem_inc(t_settled, 1)
                for s in range(TT):
                    last = nc.vector.bn_aggr(mv[:, s, :], stats[:, s, :])
                last.then_inc(t_settled, 1)
                v.wait_ge(t_settled, b * 2 + 2)
                nc.vector.tensor_scalar(var[:, :], mv[:, :, 1], EPS, None, ALU.add).then_inc(t_var, 1)

            def tail_norm(b):
                v.wait_ge(t_r0, b + 1)
                chain = Chain(v, n_chain, b * 6 + 3, 3)
                chain.link(nc.vector.tensor_tensor(r1[:, :], r0[:, :], r0[:, :], ALU.mult))
                chain.link(nc.vector.tensor_tensor(r1[:, :], r1[:, :], var[:, :], ALU.mult))
                chain.link(nc.vector.tensor_scalar(r1[:, :], r1[:, :], -0.5, 1.5, ALU.mult, ALU.add))
                nc.vector.tensor_tensor(r2[:, :], r1[:, :], r0[:, :], ALU.mult).then_inc(t_x, 1)
                v.wait_ge(t_x, b * 2 + 1)
                for s in range(TT):
                    last = nc.vector.tensor_scalar(X[:, bass.ds(b * TT + s, 1), :], res[:, s, :],
                                                   mv[:, s, 0:1], r2[:, s:s + 1], ALU.subtract, ALU.mult)
                last.then_inc(t_x, 1)

            def heads(b, q, with_front, with_tail):
                for h in range(NH):
                    k = b * NH + h
                    normalize(k, h % 2)
                    if h < NH - 2 or with_front:
                        row_max(k + 2, h % 2)
                    if with_tail and h == 3:
                        tail_res(b - 1)
                    if with_tail and h == 4:
                        tail_norm(b - 1)
                    if with_front and h == 5:
                        rope_q(b + 1)
                    if with_front and h == 8:
                        take_k(b + 1, 1 - q)
                    if with_front and h == 9:
                        take_v(b + 1, 1 - q)

            rope_q(0)
            take_k(0, 0)
            v.wait_ge(v_zero, 2)
            take_v(0, 0)
            row_max(0, 0)
            row_max(1, 1)
            steps(v, heads)
            tail_res(B - 1)
            tail_norm(B - 1)
            v.wait_ge(t_x, 2 * B)

        @block.tensor
        def _(pe):
            pe.sem_inc(h_t, 2)
            pe.sem_inc(h_pv, 2)

            def transposes(b):
                pe.wait_ge(f_xs, b + 1)
                for c in range(DC):
                    for s in range(TT):
                        last = nc.tensor.transpose(ps_m0[:, c, s * P:(s + 1) * P],
                                                   xs[:, s, c * P:(c + 1) * P], ident[:, :])
                last.then_inc(f_tr, 1)

            def project(dst, w, src, done):
                for c in range(DC):
                    for k in range(DC):
                        last = nc.tensor.matmul(dst[:, c, :], w[:, k, c * P:(c + 1) * P], src[:, k, :],
                                                start=(k == 0), stop=(k == DC - 1))
                last.then_inc(done, 1)

            def values(q):
                for s in range(TT):
                    for k in range(DC):
                        last = nc.tensor.matmul(ps_m1[:, s, :], ctxT[q][:, k, s * P:(s + 1) * P], wv[:, k, :],
                                                start=(k == 0), stop=(k == DC - 1))
                last.then_inc(f_v, 1)

            def scores(k, h, q):
                c, r, odd = h // 8, 32 * (h % 8 // 2), h % 2
                pe.wait_ge(h_exp, free(k))
                for s in range(TT):
                    last = nc.tensor.matmul(ps_s[h % 2][:, s, :], QT[q][r:r + 32, c, s * P:(s + 1) * P],
                                            KT[q][r:r + 32, odd, c, :], start=True, stop=True)
                last.then_inc(h_s, 1)

            def turn(k, h):
                pe.wait_ge(h_norm, k + 1)
                pe.wait_ge(h_pt, free(k))
                for t in range(TT):
                    for s in range(TT):
                        last = nc.tensor.transpose(ps_t[h % 2][:, t, s * P:(s + 1) * P],
                                                   prob[:, h % 2, s, t * P:(t + 1) * P], ident[:, :])
                last.then_inc(h_t, 1)

            def weigh(b, g, q, fresh):
                if g == 0 and fresh:
                    pe.wait_ge(t_o, b)
                pe.wait_ge(h_pt, made(b * NH + g * HG + HG - 1))
                for t in range(TT):
                    for j in range(HG):
                        h = g * HG + j
                        last = nc.tensor.matmul(ps_o[32 * j:32 * j + 32, g, :], V[q][:, t, h, :],
                                                probT[:, h % (2 * HG), t, :],
                                                start=(t == 0), stop=(t == TT - 1))
                last.then_inc(h_pv, 1)

            def project_out(b):
                pe.wait_ge(t_o, b + 1)
                for s in range(TT):
                    for g in range(HG):
                        last = nc.tensor.matmul(ps_m0[:, s, :], oT[:, g, s * P:(s + 1) * P], wo[:, g, :],
                                                start=(g == 0), stop=(g == HG - 1))
                last.then_inc(t_w, 1)

            def heads(b, q, with_front, with_tail):
                for h in range(NH):
                    k = b * NH + h
                    if h < NH - 2:
                        scores(k + 2, h + 2, q)
                    elif with_front:
                        scores(k + 2, h + 2 - NH, 1 - q)
                    if h % HG == 0 and h > 0:
                        weigh(b, h // HG - 1, q, with_tail)
                    if h == 0 and with_tail:
                        weigh(b - 1, NH // HG - 1, 1 - q, True)
                    turn(k, h)
                    if with_tail and h == 2:
                        project_out(b - 1)
                    if with_front and h == 4:
                        if with_tail:
                            pe.wait_ge(t_res, b)
                        transposes(b + 1)
                    if with_front and h == 6:
                        pe.wait_ge(f_qr, b + 2)
                        project(ps_m1, wq, qr, f_q)
                    if with_front and h == 7:
                        pe.wait_ge(f_kr, b + 2)
                        project(ps_m0, wk, kr, f_k)
                    if with_front and h == 8:
                        pe.wait_ge(f_qs, b + 2)
                        values(1 - q)
                    if with_front and h == 13:
                        pe.wait_ge(f_ks, b + 2)
                        pe.wait_ge(f_vs, b + 2)

            pe.wait_ge(w_got, 16 * len(loads))
            transposes(0)
            pe.wait_ge(f_qr, 1)
            project(ps_m1, wq, qr, f_q)
            pe.wait_ge(f_kr, 1)
            project(ps_m0, wk, kr, f_k)
            pe.wait_ge(f_qs, 1)
            values(0)
            pe.wait_ge(f_ks, 1)
            pe.wait_ge(f_vs, 1)
            scores(0, 0, 0)
            scores(1, 1, 0)
            steps(pe, heads)
            weigh(B - 1, NH // HG - 1, 1, True)
            project_out(B - 1)


def shared_phase(nc, dram, X, Y, logits, ident, slots_dram):
    with ExitStack() as ctx:
        def sb(name, shape, dt=F32):
            return ctx.enter_context(nc.sbuf_tensor(name, shape, dt))

        def ps(name, shape, dt=F32):
            return ctx.enter_context(nc.psum_tensor(name, shape, dt))

        def sem(name):
            return ctx.enter_context(nc.semaphore(name))

        FC = FS // P
        w1 = sb("sw1", [P, DC, 2 * FS])
        w2 = sb("sw2", [P, FC, D])
        b1 = sb("sb1", [P, 2 * FC])
        b2 = sb("sb2", [P, D])
        mult = sb("smult", [P, FC])
        wg = sb("wg", [P, DC, NE])
        xs = sb("c_xs", [P, TT, D])
        xT = [sb(f"c_xT{j}", [P, DC, L]) for j in range(2)]
        gate = sb("c_gate", [P, FC, L])
        act_T = sb("c_act", [P, FC, L])
        y_b = sb("c_y", [P, TT, D])
        zero = sb("zero", [P, D])
        ps_x = ps("c_ps_x", [P, DC, L])
        ps_u = ps("c_ps_u", [P, FC, L])
        ps_g = ps("c_ps_g", [P, FC, L])
        ps_y = ps("c_ps_y", [P, TT, D])
        ps_l = ps("c_ps_l", [P, TT, NE])
        got, scaled, zero_made, zeroed = (sem("c_" + n) for n in ("got", "scaled", "zero_made", "zeroed"))
        c_xs, c_tr, c_xT, c_up, c_gp, c_gelu, c_act, c_yp, c_y1, c_y2, c_lp, c_l = (
            sem("c_" + n) for n in
            ("xs", "tr", "xT", "up", "gp", "gelu", "act", "yp", "y1", "y2", "lp", "l"))
        loads = ((w1[:, :, :], dram["s_fc1T"].rearrange("(c p) e -> p c e", p=P)),
                 (w2[:, :, :], dram["s_fc2T"].rearrange("(c p) e -> p c e", p=P)),
                 (b1[:, :], dram["s_fc1_b"]), (mult[:, :], dram["s_mult"]),
                 (b2[:, :], dram["s_fc2_b"].to_broadcast([P, D])),
                 (wg[:, :, :], dram["gateT"].rearrange("(c p) e -> p c e", p=P)))
        block = ctx.enter_context(nc.Block())

        def steps(eng, body):
            with eng.Fori(0, B // 2 - 1) as i:
                body(i * 2, 0, True)
                body(i * 2 + 1, 1, True)
            body(B - 2, 0, True)
            body(B - 1, 1, False)

        @block.sync
        def _(sp):
            for dst, src in loads:
                sp.dma_start(dst, src).then_inc(got, 16)
            sp.wait_ge(zero_made, 1)
            sp.dma_start(slots_dram.rearrange("(i p) d -> p i d", p=P),
                         zero[:, :].unsqueeze(1).to_broadcast([P, SLOT_TILES, D])).then_inc(zeroed, 16)
            sp.wait_ge(zeroed, 16)

        @block.gpsimd
        def _(g):
            nc.gpsimd.memset(zero[:, :], 0.0).then_inc(zero_made, 1)

        @block.scalar
        def _(act):
            act.preload_act_table_set("gelu_and_others")

            def copy_x(b):
                nc.scalar.activation(xs[:, :, :], X[:, bass.ds(b * TT, TT), :], ACT.Copy).then_inc(c_xs, 1)

            def take_xT(b, q):
                act.wait_ge(c_tr, b + 1)
                nc.scalar.activation(xT[q][:, :, :], ps_x[:, :, :], ACT.Copy).then_inc(c_xT, 1)

            def body(b, q, more):
                if more:
                    copy_x(b + 1)
                act.wait_ge(c_gp, b + 1)
                act.wait_ge(c_act, b + 1)
                for c in range(FC):
                    last = nc.scalar.activation(gate[:, c, :], ps_g[:, c, :], ACT.Gelu,
                                                bias=b1[:, FC + c:FC + c + 1])
                last.then_inc(c_gelu, 1)
                if more:
                    take_xT(b + 1, 1 - q)
                act.wait_ge(c_lp, b + 1)
                nc.scalar.activation(logits[:, bass.ds(b * TT, TT), 0:NE], ps_l[:, :, :],
                                     ACT.Copy).then_inc(c_l, 1)

            act.wait_ge(got, 16 * len(loads))
            copy_x(0)
            take_xT(0, 0)
            steps(act, body)
            act.wait_ge(c_l, B)

        @block.vector
        def _(v):
            v.wait_ge(got, 16 * len(loads))
            for c in range(FC):
                last = nc.vector.tensor_scalar(w2[:, c, :], w2[:, c, :], mult[:, c:c + 1], None, ALU.mult)
            last.then_inc(scaled, 1)

            def body(b, q, more):
                v.wait_ge(c_gelu, b + 1)
                v.wait_ge(c_up, b + 1)
                for c in range(FC):
                    last = nc.vector.scalar_tensor_tensor(act_T[:, c, :], ps_u[:, c, :], b1[:, c:c + 1],
                                                          gate[:, c, :], ALU.add, ALU.mult)
                last.then_inc(c_act, 1)
                v.wait_ge(c_yp, b + 1)
                nc.vector.tensor_tensor(y_b[:, :, :], ps_y[:, :, :],
                                        b2[:, :].unsqueeze(1).to_broadcast([P, TT, D]), ALU.add).then_inc(c_y1, 1)
                v.wait_ge(c_y1, b + 1)
                at = bass.ds(b * TT, TT)
                nc.vector.tensor_tensor(Y[:, at, :], y_b[:, :, :], X[:, at, :], ALU.add).then_inc(c_y2, 1)
                v.wait_ge(c_y2, b + 1)

            steps(v, body)

        @block.tensor
        def _(pe):
            def transposes(b):
                pe.wait_ge(c_xs, b + 1)
                for c in range(DC):
                    for s in range(TT):
                        last = nc.tensor.transpose(ps_x[:, c, s * P:(s + 1) * P],
                                                   xs[:, s, c * P:(c + 1) * P], ident[:, :])
                last.then_inc(c_tr, 1)

            def up(dst, q, at, done):
                for c in range(FC):
                    for k in range(DC):
                        last = nc.tensor.matmul(dst[:, c, :], w1[:, k, at + c * P:at + (c + 1) * P],
                                                xT[q][:, k, :], start=(k == 0), stop=(k == DC - 1))
                last.then_inc(done, 1)

            def body(b, q, more):
                pe.wait_ge(c_xT, b + 1)
                pe.wait_ge(c_act, b + 1)
                up(ps_u, q, 0, c_up)
                for s in range(TT):
                    for k in range(DC):
                        last = nc.tensor.matmul(ps_l[:, s, :], xT[q][:, k, s * P:(s + 1) * P], wg[:, k, :],
                                                start=(k == 0), stop=(k == DC - 1))
                last.then_inc(c_lp, 1)
                if more:
                    transposes(b + 1)
                    pe.wait_ge(c_xT, b + 2)
                    pe.wait_ge(c_gelu, b + 1)
                    up(ps_g, 1 - q, FS, c_gp)
                pe.wait_ge(c_act, b + 2)
                for s in range(TT):
                    for k in range(FC):
                        last = nc.tensor.matmul(ps_y[:, s, :], act_T[:, k, s * P:(s + 1) * P], w2[:, k, :],
                                                start=(k == 0), stop=(k == FC - 1))
                last.then_inc(c_yp, 1)
                pe.wait_ge(c_l, b + 1)
                pe.wait_ge(c_y1, b + 1)

            pe.wait_ge(got, 16 * len(loads))
            pe.wait_ge(scaled, 1)
            pe.sem_inc(c_act, 1)
            transposes(0)
            pe.wait_ge(c_xT, 1)
            up(ps_g, 0, FS, c_gp)
            steps(pe, body)


def route_phase(nc, dram, X, logits, weights, slot_of, expert_of, slots_dram):
    with ExitStack() as ctx:
        def sb(name, shape, dt=F32):
            return ctx.enter_context(nc.sbuf_tensor(name, shape, dt))

        def sem(name):
            return ctx.enter_context(nc.semaphore(name))

        tri, ones = sb("tri", [P, P]), sb("ones", [P, P])
        iota_e = sb("iota_e", [P, NE])
        iota_m = sb("iota_m", [P, NT])
        iota_s = sb("iota_s", [1, SLOT_TILES])
        not_first = sb("not_first", [P, NE, NT])
        top = sb("top", [P, NT, 8])
        top_i = sb("top_i", [P, NT, 8], mybir.dt.uint32)
        top_f = sb("top_f", [P, NT, TOPK])
        shifted = sb("shifted", [P, NT, NE])
        exps = sb("exps", [P, NT, NE])
        top_e = sb("top_e", [P, NT, TOPK])
        total = sb("r_total", [P, NT])
        inv = sb("r_inv", [P, NT])
        top_p = sb("top_p", [P, NT, TOPK])
        hot = sb("hot", [P, TOPK, NT, NE])
        mask = sb("mask", [P, NT, NE])
        before = sb("before", [P, NT, NE])
        tile_sum = sb("tile_sum", [P, NE, NT])
        running = sb("running", [P, NE, NT])
        excl = sb("excl", [P, NE, NT])
        filled = sb("filled", [P, NE, NT])
        n_tiles = sb("n_tiles", [P, NE])
        tile_end = sb("tile_end", [P, NE])
        base = sb("base", [P, NE])
        slot = sb("slot", [P, NT, NE])
        picked = sb("picked", [P, NT, NE])
        slot_f = sb("slot_f", [P, TOPK, NT])
        past = sb("past", [1, SLOT_TILES, NE])
        exp_f = sb("exp_f", [1, SLOT_TILES])
        ps_before = ctx.enter_context(nc.psum_tensor("ps_before", [P, NT, NE], F32))
        ps_total = ctx.enter_context(nc.psum_tensor("ps_total", [P, NT, NE], F32))
        got, top_made, shift_made, exp_made, top_exp, mask_made, counted, slots_ready, scattered = (
            sem("r_" + n) for n in ("got", "top", "shift", "exp", "top_exp", "mask", "counted", "ready",
                                    "scattered"))
        own, chain_s = sem("r_own"), sem("r_chain")
        block = ctx.enter_context(nc.Block())
        loads = ((tri[:, :], dram["tri"]), (ones[:, :], dram["ones"]),
                 (iota_e[:, :], dram["iota"][0:1, 0:NE].to_broadcast([P, NE])),
                 (iota_m[:, :], dram["iota_m"].to_broadcast([P, NT])),
                 (iota_s[:, :], dram["iota"][0:1, 0:SLOT_TILES]),
                 (not_first[:, :, :].rearrange("p e t -> p (e t)"),
                  dram["not_first"].to_broadcast([P, NE * NT])))

        @block.sync
        def _(sp):
            for dst, src in loads:
                sp.dma_start(dst, src).then_inc(got, 16)

        @block.scalar
        def _(act):
            act.wait_ge(shift_made, 1)
            nc.scalar.activation(exps[:, :, :], shifted[:, :, :], ACT.Exp).then_inc(exp_made, 1)
            act.wait_ge(exp_made, 1)
            nc.scalar.activation(top_e[:, :, :], top_f[:, :, :], ACT.Exp).then_inc(top_exp, 1)

        @block.tensor
        def _(pe):
            pe.wait_ge(mask_made, 1)
            pe.wait_ge(got, 16 * len(loads))
            nc.tensor.matmul(ps_before[:, :, :], tri[:, :], mask[:, :, :], start=True, stop=True)
            nc.tensor.matmul(ps_total[:, :, :], ones[:, :], mask[:, :, :], start=True,
                             stop=True).then_inc(counted, 1)

        @block.vector
        def _(v):
            def by_token(a):
                return a.unsqueeze(2).to_broadcast([P, NT, NE])

            for t in range(NT):
                last = nc.vector.max(top[:, t, :], logits[:, t, 0:NE])
            last.then_inc(top_made, 1)
            v.wait_ge(top_made, 1)
            for t in range(NT):
                last = nc.vector.max_index(top_i[:, t, :], top[:, t, :], logits[:, t, 0:NE])
            nc.vector.tensor_tensor(top_f[:, :, :], top[:, :, 0:TOPK],
                                    top[:, :, 0:1].to_broadcast([P, NT, TOPK]), ALU.subtract)
            nc.vector.tensor_tensor(shifted[:, :, :], logits[:, :, 0:NE], top[:, :, 0:1].to_broadcast([P, NT, NE]),
                                    ALU.subtract).then_inc(shift_made, 1)
            chain = Chain(v, chain_s, 0, 26)
            v.wait_ge(top_exp, 1)
            chain.link(nc.vector.tensor_reduce(total[:, :], exps[:, :, :], AXX, ALU.add))
            chain.link(nc.vector.reciprocal(inv[:, :], total[:, :]))
            chain.link(nc.vector.tensor_tensor(top_p[:, :, :], top_e[:, :, :],
                                               inv[:, :].unsqueeze(2).to_broadcast([P, NT, TOPK]), ALU.mult))
            chain.link(nc.vector.tensor_reduce(total[:, :], top_p[:, :, :], AXX, ALU.add))
            chain.link(nc.vector.tensor_scalar(total[:, :], total[:, :], 1e-20, None, ALU.add))
            chain.link(nc.vector.reciprocal(inv[:, :], total[:, :]))
            chain.link(nc.vector.tensor_tensor(weights[:, :, :], top_p[:, :, :],
                                               inv[:, :].unsqueeze(2).to_broadcast([P, NT, TOPK]), ALU.mult))
            chain.link(nc.vector.tensor_copy(top_f[:, :, :], top_i[:, :, 0:TOPK]))
            v.wait_ge(got, 16 * len(loads))
            for j in range(TOPK):
                last = nc.vector.tensor_tensor(hot[:, j, :, :], iota_e[:, :].unsqueeze(1).to_broadcast([P, NT, NE]),
                                               top_f[:, :, j:j + 1].to_broadcast([P, NT, NE]), ALU.is_equal)
            chain.link(last)
            chain.link(nc.vector.tensor_tensor(mask[:, :, :], hot[:, 0, :, :], hot[:, 1, :, :], ALU.add))
            chain.link(nc.vector.tensor_tensor(mask[:, :, :], mask[:, :, :], hot[:, 2, :, :], ALU.add))
            v.sem_inc(mask_made, 1)
            v.wait_ge(counted, 1)
            chain.link(nc.vector.tensor_copy(tile_sum[:, :, :], ps_total[:, :, :].rearrange("p t e -> p e t")))
            chain.link(nc.vector.tensor_tensor_scan(
                running[:, :, :].rearrange("p e t -> p (e t)"), not_first[:, :, :].rearrange("p e t -> p (e t)"),
                tile_sum[:, :, :].rearrange("p e t -> p (e t)"), 0.0, ALU.mult, ALU.add))
            chain.link(nc.vector.tensor_tensor(excl[:, :, :], running[:, :, :], tile_sum[:, :, :], ALU.subtract))
            chain.link(nc.vector.tensor_tensor(
                filled[:, :, :], running[:, :, NT - 1:NT].to_broadcast([P, NE, NT]),
                iota_m[:, :].unsqueeze(1).to_broadcast([P, NE, NT]), ALU.is_gt))
            chain.link(nc.vector.tensor_reduce(n_tiles[:, :], filled[:, :, :], AXX, ALU.add))
            chain.link(nc.vector.tensor_tensor_scan(tile_end[:, :], ones[:, 0:NE], n_tiles[:, :], 0.0,
                                                    ALU.mult, ALU.add))
            chain.link(nc.vector.tensor_tensor(base[:, :], tile_end[:, :], n_tiles[:, :], ALU.subtract))
            chain.link(nc.vector.scalar_tensor_tensor(
                excl[:, :, :], base[:, :].unsqueeze(2).to_broadcast([P, NE, NT]), float(P), excl[:, :, :],
                ALU.mult, ALU.add))
            chain.link(nc.vector.tensor_tensor(slot[:, :, :], excl[:, :, :].rearrange("p e t -> p t e"),
                                               ps_before[:, :, :], ALU.add))
            for j in range(TOPK):
                chain.link(nc.vector.tensor_tensor(picked[:, :, :], slot[:, :, :], hot[:, j, :, :], ALU.mult))
                last = nc.vector.tensor_reduce(slot_f[:, j, :], picked[:, :, :], AXX, ALU.add)
                if j < TOPK - 1:
                    chain.link(last)
            last.then_inc(own, 1)
            v.wait_ge(own, 1)
            chain.link(nc.vector.tensor_copy(slot_of[:, :, :], slot_f[:, :, :]))
            v.sem_inc(slots_ready, 1)
            chain.close()
            nc.vector.tensor_tensor(past[:, :, :], iota_s[:, :].unsqueeze(2).to_broadcast([1, SLOT_TILES, NE]),
                                    tile_end[0:1, :].unsqueeze(1).to_broadcast([1, SLOT_TILES, NE]),
                                    ALU.is_ge).then_inc(own, 1)
            v.wait_ge(own, 2)
            nc.vector.tensor_reduce(exp_f[:, :], past[:, :, :], AXX, ALU.add).then_inc(own, 1)
            v.wait_ge(own, 3)
            nc.vector.tensor_scalar(expert_of[:, :], exp_f[:, :], float(NE - 1), None, ALU.min).then_inc(own, 1)
            v.wait_ge(own, 4)

        @block.gpsimd
        def _(g):
            g.wait_ge(slots_ready, 1)
            for t in range(NT):
                for j in range(TOPK):
                    g.indirect_dma_start(
                        out=slots_dram, out_offset=bass.IndirectOffsetOnAxis(ap=slot_of[:, j, t:t + 1], axis=0),
                        in_=X[:, t, :], in_offset=None).then_inc(scattered, 16)
            g.wait_ge(scattered, 16 * NT * TOPK)


def expert_phase(nc, dram, ident, expert_of, slots_dram, y_dram):
    with ExitStack() as ctx:
        def sb(name, shape, dt=F32):
            return ctx.enter_context(nc.sbuf_tensor(name, shape, dt))

        def ps(name, shape, dt=F32):
            return ctx.enter_context(nc.psum_tensor(name, shape, dt))

        def sem(name):
            return ctx.enter_context(nc.semaphore(name))

        FC = FE // P
        R = 4
        BF = mybir.dt.bfloat16
        w1 = sb("ew1", [P, NE, DC, 2 * FE])
        w2 = sb("ew2", [P, NE, FC, D])
        mult = sb("emult", [P, NE, FC])
        NB = 2 * FE + D
        NBP = NE * NB // P
        bias = sb("ebias", [P, NBP])
        rest = sb("erest", [P, NBP])
        part = sb("epart", [P, 3, NBP], BF)
        rows = sb("erows", [3, NE, NB], BF)
        ones = sb("eones", [3, P], BF)
        xg = [sb(f"xg{j}", [P, D]) for j in range(R)]
        xT = [sb(f"e_xT{j}", [P, DC, P]) for j in range(2)]
        gate = [sb(f"e_gate{j}", [P, FE]) for j in range(2)]
        act_s = [sb(f"e_act{j}", [P, FE]) for j in range(2)]
        aT = [sb(f"e_aT{j}", [P, FC, P]) for j in range(2)]
        y = [sb(f"e_y{j}", [P, D]) for j in range(R)]
        ps_x = [ps(f"e_ps_x{j}", [P, DC, P]) for j in range(2)]
        ps_h = [ps(f"e_ps_h{j}", [P, 2 * FE]) for j in range(2)]
        ps_a = [ps(f"e_ps_a{j}", [P, FC, P]) for j in range(2)]
        ps_y = [ps(f"e_ps_y{j}", [P, D]) for j in range(2)]
        got_b, got_w, scaled, b_chain, parts_out, rows_in, ones_made = (
            sem("e_" + n) for n in ("got_b", "got_w", "scaled", "b_chain", "parts_out", "rows_in", "ones_made"))
        x_in = [sem(f"e_x_in{j}") for j in range(R)]
        y_out = [sem(f"e_y_out{j}") for j in range(R)]
        e_tr, e_xT, e_h, e_gate, e_act, e_ta, e_aT, e_yp, e_y = (
            sem("e_" + n) for n in ("tr", "xT", "h", "gate", "act", "ta", "aT", "yp", "y"))
        rows_dram = nc.dram_tensor("bias_rows", (3, P, NBP), BF, kind="Internal").ap()
        block = ctx.enter_context(nc.Block())
        ROUNDS = SLOT_TILES // R

        def steps(eng, body):
            with eng.Fori(0, ROUNDS - 1) as i:
                for j in range(R):
                    body(i, j, False)
            for j in range(R):
                body(ROUNDS - 1, j, True)

        @block.sync
        def _(sp):
            sp.dma_start(bias[:, :], dram["e_bias"]).then_inc(got_b, 16)
            sp.dma_start(mult[:, :, :], dram["e_mult"]).then_inc(got_w, 16)
            w1_v = dram["fc1T"].rearrange("e (c p) f -> p e c f", p=P)
            w2_v = dram["fc2T"].rearrange("e (c p) f -> p e c f", p=P)
            for e in range(NE):
                sp.dma_start(w1[:, e, :, :], w1_v[:, e, :, :]).then_inc(got_w, 16)
                sp.dma_start(w2[:, e, :, :], w2_v[:, e, :, :]).then_inc(got_w, 16)
            for j in range(R):
                sp.dma_start(xg[j][:, :], slots_dram[j * P:(j + 1) * P, :]).then_inc(x_in[j], 16)
            sp.wait_ge(b_chain, 5)
            sp.dma_start(rows_dram.rearrange("r p n -> p r n"), part[:, :, :]).then_inc(parts_out, 16)
            sp.wait_ge(parts_out, 16)
            sp.dma_start(rows[:, :, :].rearrange("r e n -> r (e n)"),
                         rows_dram.rearrange("r p n -> r (p n)")).then_inc(rows_in, 16)

            slot_v = slots_dram.rearrange("(i p) d -> p i d", p=P)
            y_v = y_dram.rearrange("(i p) d -> p i d", p=P)

            def step(i, j, last):
                t = i * R + j
                sp.wait_ge(e_y, t + 1)
                sp.dma_start(y_v[:, bass.ds(t, 1), :], y[j][:, :].unsqueeze(1)).then_inc(y_out[j], 16)
                if not last:
                    sp.dma_start(xg[j][:, :].unsqueeze(1), slot_v[:, bass.ds(t + R, 1), :]).then_inc(x_in[j], 16)

            steps(sp, step)
            for j in range(R):
                sp.wait_ge(y_out[j], 16 * ROUNDS + 16)

        @block.gpsimd
        def _(g):
            nc.gpsimd.memset(ones[:, :], 1.0).then_inc(ones_made, 1)
            g.wait_ge(got_w, 16 * (2 * NE + 1))
            nc.gpsimd.tensor_tensor(
                w2[:, :, :, :].rearrange("p e c f -> p (e c) f"), w2[:, :, :, :].rearrange("p e c f -> p (e c) f"),
                mult[:, :, :].rearrange("p e c -> p (e c)").unsqueeze(2).to_broadcast([P, NE * FC, D]),
                ALU.mult).then_inc(scaled, 1)

        @block.scalar
        def _(act):
            act.preload_act_table_set("gelu_and_others")
            for j in range(R):
                act.sem_inc(y_out[j], 16)

            def take_x(t, j):
                act.wait_ge(e_tr, t + 1)
                nc.scalar.activation(xT[j % 2][:, :, :], ps_x[j % 2][:, :, :], ACT.Copy).then_inc(e_xT, 1)

            def gelu(t, j):
                act.wait_ge(e_h, t + 1)
                nc.scalar.activation(gate[j % 2][:, :], ps_h[j % 2][:, FE:], ACT.Gelu).then_inc(e_gate, 1)

            def step(i, j, last):
                t = i * R + j
                if not last or j < R - 2:
                    take_x(t + 2, j)
                if not last or j < R - 1:
                    gelu(t + 1, j + 1)
                act.wait_ge(e_yp, t + 1)
                act.wait_ge(y_out[j], i * 16 + 16)
                nc.scalar.activation(y[j][:, :], ps_y[j % 2][:, :], ACT.Copy).then_inc(e_y, 1)

            take_x(0, 0)
            take_x(1, 1)
            gelu(0, 0)
            steps(act, step)

        @block.vector
        def _(v):
            v.wait_ge(got_b, 16)
            chain = Chain(v, b_chain, 0, 5)
            chain.link(nc.vector.tensor_copy(part[:, 0, :], bias[:, :]))
            chain.link(nc.vector.tensor_tensor(rest[:, :], bias[:, :], part[:, 0, :], ALU.subtract))
            chain.link(nc.vector.tensor_copy(part[:, 1, :], rest[:, :]))
            chain.link(nc.vector.tensor_tensor(rest[:, :], rest[:, :], part[:, 1, :], ALU.subtract))
            chain.link(nc.vector.tensor_copy(part[:, 2, :], rest[:, :]))
            chain.close()

            def multiply(t, j):
                v.wait_ge(e_gate, t + 1)
                nc.vector.tensor_tensor(act_s[j % 2][:, :], ps_h[j % 2][:, 0:FE], gate[j % 2][:, :],
                                        ALU.mult).then_inc(e_act, 1)

            def step(i, j, last):
                t = i * R + j
                v.wait_ge(e_ta, t + 1)
                nc.vector.tensor_copy(aT[j % 2][:, :, :], ps_a[j % 2][:, :, :]).then_inc(e_aT, 1)
                if not last or j < R - 1:
                    multiply(t + 1, j + 1)

            multiply(0, 0)
            steps(v, step)

        @block.tensor
        def _(pe):
            pe.wait_ge(got_w, 16 * (2 * NE + 1))
            pe.wait_ge(scaled, 1)
            pe.wait_ge(rows_in, 16)
            pe.wait_ge(ones_made, 1)

            def turn_x(t, round_, j):
                pe.wait_ge(x_in[j], round_ * 16 + 16)
                for c in range(DC):
                    last = nc.tensor.transpose(ps_x[j % 2][:, c, :], xg[j][:, c * P:(c + 1) * P], ident[:, :])
                last.then_inc(e_tr, 1)

            def expert(t):
                return pe.value_load(expert_of[0:1, bass.ds(t, 1)], min_val=0, max_val=NE - 1)

            def up(t, j):
                e = expert(t)
                pe.wait_ge(e_xT, t + 1)
                nc.tensor.matmul(ps_h[j % 2][:, :], ones[:, :], rows[:, bass.ds(e, 1), 0:2 * FE],
                                 start=True, stop=False)
                for k in range(DC):
                    last = nc.tensor.matmul(ps_h[j % 2][:, :], xT[j % 2][:, k, :], w1[:, bass.ds(e, 1), k, :],
                                            start=False, stop=(k == DC - 1))
                last.then_inc(e_h, 1)

            def step(i, j, last):
                t = i * R + j
                pe.wait_ge(e_act, t + 1)
                for c in range(FC):
                    done = nc.tensor.transpose(ps_a[j % 2][:, c, :], act_s[j % 2][:, c * P:(c + 1) * P], ident[:, :])
                done.then_inc(e_ta, 1)
                if not last or j < R - 2:
                    turn_x(t + 2, i + (j + 2) // R, (j + 2) % R)
                if not last or j < R - 1:
                    up(t + 1, (j + 1) % R)
                e = expert(t)
                pe.wait_ge(e_aT, t + 1)
                nc.tensor.matmul(ps_y[j % 2][:, :], ones[:, :], rows[:, bass.ds(e, 1), 2 * FE:],
                                 start=True, stop=False)
                for k in range(FC):
                    done = nc.tensor.matmul(ps_y[j % 2][:, :], aT[j % 2][:, k, :], w2[:, bass.ds(e, 1), k, :],
                                            start=False, stop=(k == FC - 1))
                done.then_inc(e_yp, 1)

            turn_x(0, 0, 0)
            turn_x(1, 0, 1)
            up(0, 0)
            steps(pe, step)


def combine_phase(nc, dram, Y, weights, slot_of, y_dram, out):
    with ExitStack() as ctx:
        def sb(name, shape, dt=F32):
            return ctx.enter_context(nc.sbuf_tensor(name, shape, dt))

        def sem(name):
            return ctx.enter_context(nc.semaphore(name))

        R = 8
        rows = sb("d_rows", [P, R, TOPK, D])
        stats, mv = sb("d_stats", [P, NT, 6]), sb("d_mv", [P, NT, 2])
        var, root, r0, r1, r2 = (sb("d_" + n, [P, NT]) for n in ("var", "root", "r0", "r1", "r2"))
        got = [sem(f"d_got{r}") for r in range(R)]
        used, chain_s, var_made, root_made, normed, stored, settled = (
            sem("d_" + n) for n in ("used", "chain", "var", "root", "normed", "stored", "settled"))
        block = ctx.enter_context(nc.Block())

        @block.gpsimd
        def _(g):
            for t in range(NT):
                if t >= R:
                    g.wait_ge(used, t - R + 1)
                for j in range(TOPK):
                    g.indirect_dma_start(
                        out=rows[:, t % R, j, :], out_offset=None, in_=y_dram,
                        in_offset=bass.IndirectOffsetOnAxis(ap=slot_of[:, j, t:t + 1], axis=0)).then_inc(
                            got[t % R], 16)

        @block.scalar
        def _(act):
            act.wait_ge(var_made, 1)
            nc.scalar.activation(root[:, :], var[:, :], ACT.Sqrt).then_inc(root_made, 1)

        @block.vector
        def _(v):
            chain = Chain(v, chain_s, 0, TOPK * NT + 2 + 4)
            for t in range(NT):
                v.wait_ge(got[t % R], 16 * TOPK * (t // R + 1))
                for j in range(TOPK):
                    last = nc.vector.scalar_tensor_tensor(Y[:, t, :], rows[:, t % R, j, :], weights[:, t, j:j + 1],
                                                          Y[:, t, :], ALU.mult, ALU.add)
                    chain.link(last)
                v.sem_inc(used, 1)
                nc.vector.bn_stats(stats[:, t, :], Y[:, t, :]).then_inc(settled, 1)
            v.wait_ge(settled, NT)
            for t in range(NT):
                last = nc.vector.bn_aggr(mv[:, t, :], stats[:, t, :])
            chain.link(last)
            chain.link(nc.vector.tensor_scalar(var[:, :], mv[:, :, 1], EPS, None, ALU.add))
            v.sem_inc(var_made, 1)
            v.wait_ge(root_made, 1)
            chain.link(nc.vector.reciprocal(r0[:, :], root[:, :]))
            chain.link(nc.vector.tensor_tensor(r1[:, :], r0[:, :], r0[:, :], ALU.mult))
            chain.link(nc.vector.tensor_tensor(r1[:, :], r1[:, :], var[:, :], ALU.mult))
            chain.link(nc.vector.tensor_scalar(r1[:, :], r1[:, :], -0.5, 1.5, ALU.mult, ALU.add))
            chain.close()
            nc.vector.tensor_tensor(r2[:, :], r1[:, :], r0[:, :], ALU.mult).then_inc(settled, 1)
            v.wait_ge(settled, NT + 1)
            for t in range(NT):
                nc.vector.tensor_scalar(Y[:, t, :], Y[:, t, :], mv[:, t, 0:1], r2[:, t:t + 1],
                                        ALU.subtract, ALU.mult).then_inc(normed, 1)

        @block.sync
        def _(sp):
            o = out.rearrange("b (s p) d -> p (b s) d", p=P)
            for q in range(4):
                sp.wait_ge(normed, (q + 1) * NT // 4)
                part = slice(q * NT // 4, (q + 1) * NT // 4)
                sp.dma_start(o[:, part, :], Y[:, part, :]).then_inc(stored, 16)
            sp.wait_ge(stored, 16 * 4)


def load_consts(nc, dram, ident):
    with nc.semaphore("ident_in") as got, nc.Block() as block:
        @block.sync
        def _(sp):
            sp.dma_start(ident[:, :], dram["ident"]).then_inc(got, 16)
            sp.wait_ge(got, 16)


def build(nc, dram, out):
    slots_dram = nc.dram_tensor("slot_rows", (SLOT_TILES * P, D), F32, kind="Internal").ap()
    y_dram = nc.dram_tensor("slot_results", (SLOT_TILES * P, D), F32, kind="Internal").ap()
    with ExitStack() as ctx:
        def sb(name, shape, dt=F32):
            return ctx.enter_context(nc.sbuf_tensor(name, shape, dt))

        ident = sb("ident", [P, P])
        Y = sb("Y", [P, NT, D])
        weights = sb("weights", [P, NT, TOPK])
        slot_of = sb("slot_of", [P, TOPK, NT], mybir.dt.uint32)
        expert_of = sb("expert_of", [1, SLOT_TILES], mybir.dt.int32)
        load_consts(nc, dram, ident)
        with nc.sbuf_tensor("X", [P, NT, D], F32) as X, nc.sbuf_tensor("logits", [P, NT, 16], F32) as logits:
            mamba_phase(nc, dram, X, Y, ident)
            attention_phase(nc, dram, X, ident)
            shared_phase(nc, dram, X, Y, logits, ident, slots_dram)
            route_phase(nc, dram, X, logits, weights, slot_of, expert_of, slots_dram)
        expert_phase(nc, dram, ident, expert_of, slots_dram, y_dram)
        combine_phase(nc, dram, Y, weights, slot_of, y_dram, out)


def kernel(**inputs):
    import numpy as _np
    import concourse.bacc as _bacc
    from concourse import mybir as _mybir
    from concourse.bass_utils import run_bass_kernel_spmd as _run

    i = {k: _np.asarray(a) for k, a in inputs.items()}

    def col(a):
        return a.reshape(-1, P, *a.shape[1:]).swapaxes(0, 1)

    def pad_heads(a):
        return _np.concatenate([a.reshape(NH, DK, D), _np.zeros((NH, 32 - DK, D), a.dtype)], 1).reshape(-1, D)

    theta = _np.float32(10000.0) ** (_np.float32(-2.0) * _np.arange(D // 2, dtype=_np.float32) / _np.float32(D))
    angle = _np.arange(1, L + 1, dtype=_np.float32)[:, None] * theta
    cos, sin = (_np.repeat(f(angle), 2, axis=-1).astype(_np.float32) for f in (_np.cos, _np.sin))
    odd_head = (_np.arange(P)[:, None] // DK % 2).astype(_np.float32)
    arrays = {
        "x": i["x"], "norm_w": col(i["L0_attn_norm_w"]),
        "in_wT": i["L0_attn_in_w"].T, "skip_wT": i["L0_attn_skip_w"].T,
        "conv_w": col(i["L0_attn_conv_w"][:, 0, :]), "conv_b": col(i["L0_attn_conv_b"]),
        "dbc_wT": _np.concatenate([i["L0_attn_Wd1"]] + [i["L0_attn_WB"], i["L0_attn_WC"]] * PARTS).T,
        "Wd2T": i["L0_attn_Wd2_w"].T, "Wd2_b": col(i["L0_attn_Wd2_b"]),
        "A_log": col(i["L0_attn_A_log"]), "W_D": col(i["L0_attn_W_D"]), "out_wT": i["L0_attn_out_w"].T,
        "pick": _np.tile(_np.eye(NBC, dtype=_np.float32), (PARTS, 1)),
        "ident": _np.eye(P, dtype=_np.float32),
        "s_fc1T": i["L0_ffn_s_fc1_w"].T, "s_fc2T": i["L0_ffn_s_fc2_w"].T,
        "s_fc1_b": col(i["L0_ffn_s_fc1_b"]), "s_mult": col(i["L0_ffn_s_geglu_mult"]),
        "s_fc2_b": i["L0_ffn_s_fc2_b"][None], "gateT": i["L0_ffn_gate_w"].T,
        "fc1T": i["L0_ffn_fc1_w"].swapaxes(1, 2), "fc2T": i["L0_ffn_fc2_w"].swapaxes(1, 2),
        "e_bias": _np.concatenate([i["L0_ffn_fc1_b"], i["L0_ffn_fc2_b"]], 1).reshape(P, -1),
        "e_mult": i["L0_ffn_geglu_mult"].reshape(NE, FE // P, P).transpose(2, 0, 1),
        "tri": _np.triu(_np.ones((P, P), _np.float32), 1), "ones": _np.ones((P, P), _np.float32),
        "iota": _np.arange(P, dtype=_np.float32)[None], "iota_m": _np.arange(NT, dtype=_np.float32)[None] * P,
        "not_first": _np.tile((_np.arange(NT) > 0).astype(_np.float32), NE)[None],
        "ctxT": i["ctx_1024"].transpose(0, 2, 1),
        "WqT": i["L0_xattn_Wq_w"].T, "WkT": i["L0_xattn_Wk_w"].T, "WvT": i["L0_xattn_Wv_w"].T,
        "WoT": pad_heads(i["L0_xattn_Wo_w"].T),
        "bq": col(i["L0_xattn_Wq_b"]), "bk": col(i["L0_xattn_Wk_b"]),
        "bv": i["L0_xattn_Wv_b"][None], "bo": i["L0_xattn_Wo_b"][None],
        "head_even": _np.repeat(1 - odd_head, DC, axis=1), "head_odd": _np.repeat(odd_head, DC, axis=1),
        "cosT": cos.T, "sinT": _np.concatenate([-sin.T[:D // 2], sin.T[D // 2:]]),
    }
    arrays = {k: _np.ascontiguousarray(a) for k, a in arrays.items()}
    nc = _bacc.Bacc("TRN2", target_bir_lowering=False, num_devices=1)
    dram = {k: nc.dram_tensor(f"in_{k}", a.shape, _mybir.dt.from_np(a.dtype), kind="ExternalInput").ap()
            for k, a in arrays.items()}
    out = nc.dram_tensor("out_0", (B, L, D), _mybir.dt.float32, kind="ExternalOutput").ap()
    build(nc, dram, out)
    r = _run(nc, [{f"in_{k}": a for k, a in arrays.items()}], core_ids=[0])
    return r.results[0]["out_0"]
```

```python
import numpy as np
import concourse.bass as bass
from concourse import mybir
from contextlib import ExitStack

F32 = mybir.dt.float32
BF16 = mybir.dt.bfloat16
ALU = mybir.AluOpType
ACT = mybir.ActivationFunctionType
AXX = mybir.AxisListType.X

P = 128
B, L, D = 16, 256, 256
T = B * L
TT = L // P
NT = T // P
DC = D // P
EI = 512
EC = EI // P
NS = 16
DD = 64
TAPS = 4
NBC = 2 * NS
RING = 4
LEAD = RING - 1
PARTS = 3
EPS = 1e-5
NE, TOPK, FE, FS = 15, 3, 256, 512
FEC, FSC = FE // P, FS // P
NB = 2 * FE + D
NBP = NE * NB // P
SLOT_TILES = (T * TOPK // P + NE + 1) // 2 * 2
NH = 16
DK = D // NH
HC = NH // DC
HG = 4
SCALE = DK ** -0.5
EXP_LN = "natural_log_exp_and_others"


class Chain:

    def __init__(self, eng, sem, base, per):
        self.eng, self.sem, self.base, self.per, self.n = eng, sem, base, per, 0

    def link(self, ins):
        self.n += 1
        ins.then_inc(self.sem, 1)
        self.eng.wait_ge(self.sem, self.base + self.n)

    def close(self):
        assert self.n == self.per, (self.n, self.per)


def mamba_phase(nc, dram, X, ident):
    with ExitStack() as ctx:
        def sb(name, shape, dt=F32):
            return ctx.enter_context(nc.sbuf_tensor(name, shape, dt))

        def ps(name, shape, dt=F32):
            return ctx.enter_context(nc.psum_tensor(name, shape, dt))

        def sem(name):
            return ctx.enter_context(nc.semaphore(name))

        w_in = sb("w_in", [P, DC, EI])
        w_skip = sb("w_skip", [P, DC, EI])
        w_dbc = sb("w_dbc", [P, EC, DD + PARTS * NBC])
        pick_f = sb("pick_f", [PARTS * NBC, NBC])
        pick = sb("pick", [PARTS * NBC, NBC], BF16)
        w_d2 = sb("w_d2", [DD, EI])
        w_out = sb("w_out", [P, EC, D])
        norm_w = sb("norm_w", [P, DC])
        conv_w = sb("conv_w", [P, EC, TAPS])
        conv_b = sb("conv_b", [P, EC])
        d2_b = sb("d2_b", [P, EC])
        w_D = sb("w_D", [P, EC])
        a_log = sb("a_log", [P, EC, NS])
        a_neg = sb("a_neg", [P, EC, NS])
        conv_diag = sb("conv_diag", [P, EC, TAPS, P])
        d_diag = sb("d_diag", [P, EC, P])
        x_stats = sb("x_stats", [P, NT, 6])
        x_mv = sb("x_mv", [P, NT, 2])
        ms = sb("ms", [P, NT])
        rstd = sb("rstd", [P, NT])
        nt1 = sb("nt1", [P, NT])
        nt2 = sb("nt2", [P, NT])
        xn = sb("xn", [P, TT, D])
        xnT = sb("xnT", [P, DC, L])
        xin = sb("xin", [P, EC, TAPS - 1 + L])
        skip_raw = sb("skip_raw", [P, EC, L])
        u = [sb(f"u{j}", [P, EC, L]) for j in range(2)]
        skip = [sb(f"skip{j}", [P, EC, L]) for j in range(2)]
        dlow = sb("dlow", [DD, L])
        bc = sb("bc", [PARTS * NBC, L])
        bc_rest = sb("bc_rest", [PARTS * NBC, L])
        bc_mid = sb("bc_mid", [PARTS * NBC, L], BF16)
        bc_parts = [sb(f"bc_parts{j}", [PARTS * NBC, L], BF16) for j in range(2)]
        delta = [sb(f"delta{j}", [P, EC, L]) for j in range(2)]
        dx = [sb(f"dx{j}", [P, EC, L]) for j in range(2)]
        z = sb("z", [P, EC, L])
        zmiss = sb("zmiss", [P, EC, L])
        zabs = sb("zabs", [P, EC, L])
        zexp = sb("zexp", [P, EC, L])
        zln = sb("zln", [P, EC, L])
        zcor = sb("zcor", [P, EC, L])
        bc_all = sb("bc_all", [P, RING, 2, L])
        decay = sb("decay", [P, RING, EC, L])
        inject = sb("inject", [P, RING, EC, L])
        h = sb("h", [P, 2, EC, L])
        hc = sb("hc", [P, 2, EC, L])
        y_gated = sb("y_gated", [P, EC, L])
        res = sb("res", [P, TT, D])
        stats = sb("stats", [P, TT, 6])
        mv = sb("mv", [P, TT, 2])
        var = sb("var", [P, TT])
        ln_var = sb("ln_var", [P, TT])
        r0 = sb("r0", [P, TT])
        r1 = sb("r1", [P, TT])
        r2 = sb("r2", [P, TT])

        ps_tr = ps("ps_tr", [P, DC, L])
        ps_pr = ps("ps_pr", [P, EC, L])
        ps_misc = ps("ps_misc", [P, TT * D])
        ps_bc = [ps(f"ps_bc{j}", [P, 2, L]) for j in range(2)]
        ps_y = ps("ps_y", [P, EC, L])

        x_first, x_in, w_first, w_loaded = (sem(n) for n in ("x_first", "x_in", "w_first", "w_loaded"))
        diag_made, rstd_made, ms_made, root_made, exp_a = (
            sem(n) for n in ("diag_made", "rstd_made", "ms_made", "root_made", "exp_a"))
        pads_zero = sem("pads_zero")
        init_chain = sem("init_chain")
        a_made = sem("a_made")
        f_xn, f_tr, f_xnT, f_in, f_xin, f_skip, f_skip_raw, f_conv, f_u = (
            sem("f_" + n) for n in ("xn", "tr", "xnT", "in", "xin", "skip", "skip_raw", "conv", "u"))
        f_dbc, f_dbc_sb, f_z, f_zsb, f_miss, f_zabs, f_zexp, f_zln, f_cor, f_delta, f_dx, f_bc, f_split = (
            sem("f_" + n) for n in
            ("dbc", "dbc_sb", "z", "zsb", "miss", "zabs", "zexp", "zln", "cor", "delta", "dx", "bc", "split"))
        z_chain = sem("z_chain")
        s_bc, s_bc_all, s_decay, s_inject, s_h, s_hc, s_sum = (
            sem("s_" + n) for n in ("bc", "bc_all", "decay", "inject", "h", "hc", "sum"))
        y_done, y_gated_done, out_done, res_free, ln_var_made, r0_made, var_made, x_made = (
            sem(n) for n in ("y_done", "y_gated_done", "out_done", "res_free", "ln_var_made", "r0_made",
                             "var_made", "x_made"))
        d_chain, s_chain, settled = sem("d_chain"), sem("s_chain"), sem("settled")

        def made(k):
            return k + 1 + RING

        def free(k, ring=RING):
            return k + 1 + RING - ring

        block = ctx.enter_context(nc.Block())
        FIRST, REST = slice(0, NT // 4), slice(NT // 4, NT)
        W_LATER = 10

        def steps(eng, body):
            body(0, 0, True, True, False)
            with eng.Fori(0, B // 2 - 2) as i:
                body(i * 2 + 1, 1, True, True, True)
                body(i * 2 + 2, 0, True, True, True)
            body(B - 3, 1, True, True, True)
            body(B - 2, 0, False, True, True)
            body(B - 1, 1, False, False, True)

        def ahead(state, b, q, n, more):
            if n + LEAD < NS:
                state(b, q, n + LEAD)
            elif more:
                state(b + 1, 1 - q, n + LEAD - NS)

        @block.sync
        def _(sp):
            x_t = dram["x"].rearrange("b (s p) d -> p (b s) d", p=P)
            for q in range(4):
                sp.dma_start(X[:, q * NT // 4:(q + 1) * NT // 4, :],
                             x_t[:, q * NT // 4:(q + 1) * NT // 4, :]).then_inc(x_in if q else x_first, 16)

        @block.gpsimd
        def _(g):
            nc.gpsimd.memset(xin[:, :, 0:TAPS - 1], 0.0).then_inc(pads_zero, 1)
            nc.gpsimd.memset(decay[:, :, :, 0:1], 0.0).then_inc(pads_zero, 1)
            g.sem_inc(s_inject, RING)

            def front(b, q):
                g.wait_ge(f_cor, b + 1)
                nc.gpsimd.tensor_tensor(zmiss[:, :, :], zexp[:, :, :], zcor[:, :, :],
                                        ALU.subtract).then_inc(f_miss, 1)

            def state(b, q, n):
                k = b * NS + n
                if n == 0:
                    g.wait_ge(f_dx, b + 1)
                g.wait_ge(s_bc_all, made(k))
                g.wait_ge(s_h, free(k))
                nc.gpsimd.tensor_tensor(
                    inject[:, n % RING, :, :], dx[q][:, :, :],
                    bc_all[:, n % RING, 0, :].unsqueeze(1).to_broadcast([P, EC, L]),
                    ALU.mult).then_inc(s_inject, 1)

            def scan(b, q, with_entry, with_front, with_tail):
                for n in range(NS):
                    ahead(state, b, q, n, with_front)
                    if with_front and n == 11:
                        front(b + 1, 1 - q)

            front(0, 0)
            for n in range(LEAD):
                state(0, 0, n)
            steps(g, scan)

        @block.scalar
        def _(act):
            loads = ((norm_w[:, :], dram["norm_w"]),
                     (w_in[:, :, :], dram["in_wT"].rearrange("(c p) e -> p c e", p=P)),
                     (w_skip[:, :, :], dram["skip_wT"].rearrange("(c p) e -> p c e", p=P)),
                     (conv_w[:, :, :], dram["conv_w"]),
                     (conv_b[:, :], dram["conv_b"]),
                     (w_D[:, :], dram["W_D"]),
                     (w_dbc[:, :, :], dram["dbc_wT"].rearrange("(c p) r -> p c r", p=P)),
                     (w_d2[:, :], dram["Wd2T"]),
                     (d2_b[:, :], dram["Wd2_b"]),
                     (a_log[:, :, :], dram["A_log"]),
                     (pick_f[:, :], dram["pick"]),
                     (w_out[:, :, :], dram["out_wT"].rearrange("(c p) d -> p c d", p=P)))
            for n, (dst, src) in enumerate(loads):
                act.dma_start(dst, src).then_inc(w_first if n < 2 else w_loaded, 16)
            act.sem_inc(s_bc_all, RING)
            act.sem_inc(s_decay, RING)
            act.preload_act_table_set(EXP_LN)

            def root(part, n):
                act.wait_ge(ms_made, n + 1)
                nc.scalar.activation(nt2[:, part], ms[:, part], ACT.Ln).then_inc(root_made, 1)
                act.wait_ge(root_made, n * 2 + 1)
                nc.scalar.activation(nt2[:, part], nt2[:, part], ACT.Exp, scale=-0.5).then_inc(root_made, 1)

            def norm_x(b):
                for s in range(TT):
                    t = b * TT + s
                    last = nc.scalar.activation(xn[:, s, :], X[:, bass.ds(t, 1), :], ACT.Copy,
                                                scale=rstd[:, bass.ds(t, 1)])
                last.then_inc(f_xn, 1)

            def scale_xT(b):
                act.wait_ge(f_tr, b + 1)
                for c in range(DC):
                    last = nc.scalar.activation(xnT[:, c, :], ps_tr[:, c, :], ACT.Copy,
                                                scale=norm_w[:, c:c + 1])
                last.then_inc(f_xnT, 1)

            def take_xin(b, banks=(0, 2)):
                for c in banks:
                    act.wait_ge(f_in, b * 2 + c // 2 + 1)
                    nc.scalar.activation(xin[:, c:c + 2, TAPS - 1:], ps_pr[:, c:c + 2, :],
                                         ACT.Copy).then_inc(f_xin, 1)

            def take_skip(b, banks=(0, 2)):
                for c in banks:
                    act.wait_ge(f_skip, b * 2 + c // 2 + 1)
                    nc.scalar.activation(skip_raw[:, c:c + 2, :], ps_pr[:, c:c + 2, :],
                                         ACT.Copy).then_inc(f_skip_raw, 1)

            def silus(b, q):
                act.preload_act_table_set("silu_and_others")
                act.wait_ge(f_skip_raw, b * 2 + 2)
                for c in range(EC):
                    if c % 2 == 0:
                        act.wait_ge(f_conv, b * 2 + c // 2 + 1)
                    nc.scalar.activation(u[q][:, c, :], ps_pr[:, c, :], ACT.Silu,
                                         bias=conv_b[:, c:c + 1]).then_inc(f_u, 1)
                nc.scalar.activation(skip[q][:, :, :], skip_raw[:, :, :], ACT.Silu).then_inc(f_u, 1)
                act.preload_act_table_set(EXP_LN)

            def take_dbc(b, q):
                act.wait_ge(f_dbc, b + 1)
                nc.scalar.activation(bc[:, :], ps_misc[0:PARTS * NBC, L:], ACT.Copy).then_inc(f_bc, 1)
                nc.scalar.activation(dlow[:, :], ps_misc[0:DD, 0:L], ACT.Copy).then_inc(f_dbc_sb, 1)

            def softplus(b):
                act.wait_ge(f_zsb, b + 1)
                nc.scalar.activation(zabs[:, :, :], z[:, :, :], ACT.Abs).then_inc(f_zabs, 1)
                act.wait_ge(f_zabs, b + 1)
                nc.scalar.activation(zexp[:, :, :], zabs[:, :, :], ACT.Exp, scale=-1.0).then_inc(f_zexp, 1)
                act.wait_ge(f_zexp, b + 1)
                nc.scalar.activation(zln[:, :, :], zexp[:, :, :], ACT.Ln, bias=1.0).then_inc(f_zln, 1)

            def layernorm_root(b):
                act.wait_ge(var_made, b + 1)
                nc.scalar.activation(ln_var[:, :], var[:, :], ACT.Ln).then_inc(ln_var_made, 1)
                act.wait_ge(ln_var_made, b + 1)
                nc.scalar.activation(r0[:, :], ln_var[:, :], ACT.Exp, scale=-0.5).then_inc(r0_made, 1)

            def state(b, q, n):
                k = b * NS + n
                act.wait_ge(s_bc, k + 1)
                act.wait_ge(s_inject, free(k))
                act.wait_ge(s_hc, free(k))
                nc.scalar.activation(bc_all[:, n % RING, :, :], ps_bc[n % 2][:, :, :],
                                     ACT.Copy).then_inc(s_bc_all, 1)
                if n == 0:
                    act.wait_ge(f_delta, b + 1)
                act.wait_ge(s_h, free(k))
                for c in range(EC):
                    last = nc.scalar.activation(decay[:, n % RING, c, 1:], delta[q][:, c, 1:], ACT.Exp,
                                                scale=a_neg[:, c, n:n + 1])
                last.then_inc(s_decay, 1)

            def scan(b, q, with_entry, with_front, with_tail):
                for n in range(NS):
                    ahead(state, b, q, n, with_front)
                    if with_entry and n == 2:
                        norm_x(b + 2)
                    if with_entry and n == 4:
                        scale_xT(b + 2)
                    if with_tail and n == 4:
                        layernorm_root(b - 1)
                    if with_front and n == 5:
                        silus(b + 1, 1 - q)
                    if with_entry and n == 7:
                        take_xin(b + 2, (0,))
                    if with_front and n == 8:
                        take_dbc(b + 1, 1 - q)
                    if with_entry and n == 8:
                        take_xin(b + 2, (2,))
                    if with_front and n == 10:
                        softplus(b + 1)
                    if with_entry and n == 12:
                        take_skip(b + 2, (0,))
                    if with_entry and n == 13:
                        take_skip(b + 2, (2,))

            root(FIRST, 0)
            act.wait_ge(rstd_made, 1)
            norm_x(0)
            act.wait_ge(w_first, 16 * 2)
            scale_xT(0)
            act.wait_ge(w_loaded, 16 * (len(loads) - 2))
            nc.scalar.activation(a_neg[:, :, :], a_log[:, :, :], ACT.Exp).then_inc(exp_a, 1)
            take_xin(0)
            take_skip(0)
            silus(0, 0)
            norm_x(1)
            take_dbc(0, 0)
            scale_xT(1)
            take_xin(1)
            softplus(0)
            act.wait_ge(a_made, 1)
            for n in range(LEAD):
                state(0, 0, n)
            take_skip(1)
            root(REST, 1)
            act.wait_ge(rstd_made, 2)
            steps(act, scan)
            layernorm_root(B - 1)

        @block.vector
        def _(v):
            v.sem_inc(s_h, RING)
            v.sem_inc(s_hc, RING)
            v.sem_inc(y_gated_done, 1)

            def mean_square(part, n):
                chain = Chain(v, init_chain, n * 6, 3)
                v.wait_ge(x_in if n else x_first, 16 * 3 if n else 16)
                for t in range(part.start, part.stop):
                    last = nc.vector.bn_stats(x_stats[:, t, :], X[:, t, :])
                chain.link(last)
                for t in range(part.start, part.stop):
                    last = nc.vector.bn_aggr(x_mv[:, t, :], x_stats[:, t, :])
                chain.link(last)
                chain.link(nc.vector.tensor_tensor(nt1[:, part], x_mv[:, part, 0], x_mv[:, part, 0], ALU.mult))
                chain.close()
                nc.vector.scalar_tensor_tensor(ms[:, part], nt1[:, part], EPS, x_mv[:, part, 1],
                                               ALU.add, ALU.add).then_inc(ms_made, 1)

            def refine(part, n):
                v.wait_ge(root_made, n * 2 + 2)
                chain = Chain(v, init_chain, n * 6 + 3, 3)
                chain.link(nc.vector.tensor_tensor(nt1[:, part], nt2[:, part], nt2[:, part], ALU.mult))
                chain.link(nc.vector.tensor_tensor(nt1[:, part], nt1[:, part], ms[:, part], ALU.mult))
                chain.link(nc.vector.tensor_scalar(nt1[:, part], nt1[:, part], -0.5, 1.5, ALU.mult, ALU.add))
                chain.close()
                nc.vector.tensor_tensor(rstd[:, part], nt1[:, part], nt2[:, part], ALU.mult).then_inc(rstd_made, 1)

            mean_square(FIRST, 0)
            refine(FIRST, 0)
            v.wait_ge(w_loaded, 16 * W_LATER)
            nc.vector.tensor_copy(pick[:, :], pick_f[:, :])
            for c in range(EC):
                for k in range(TAPS):
                    nc.vector.tensor_scalar(conv_diag[:, c, k, :], ident[:, :], conv_w[:, c, k:k + 1], None,
                                            ALU.mult)
                last = nc.vector.tensor_scalar(d_diag[:, c, :], ident[:, :], w_D[:, c:c + 1], None, ALU.mult)
            last.then_inc(diag_made, 1)
            v.wait_ge(exp_a, 1)
            nc.vector.tensor_scalar(a_neg[:, :, :], a_neg[:, :, :], -1.0, None, ALU.mult).then_inc(a_made, 1)
            mean_square(REST, 1)

            def take_z(b):
                v.wait_ge(f_z, b + 1)
                for c in range(EC):
                    last = nc.vector.tensor_scalar(z[:, c, :], ps_pr[:, c, :], d2_b[:, c:c + 1], None, ALU.add)
                last.then_inc(f_zsb, 1)

            def split_bc(b, q):
                v.wait_ge(f_bc, b + 1)
                chain = Chain(v, s_chain, b * 4, 4)
                chain.link(nc.vector.tensor_copy(bc_parts[q][:, :], bc[:, :]))
                chain.link(nc.vector.tensor_tensor(bc_rest[:, :], bc[:, :], bc_parts[q][:, :], ALU.subtract))
                mid, low = slice(NBC, 2 * NBC), slice(2 * NBC, 3 * NBC)
                chain.link(nc.vector.tensor_copy(bc_parts[q][mid, :], bc_rest[mid, :]))
                chain.link(nc.vector.tensor_copy(bc_mid[low, :], bc_rest[low, :]))
                chain.close()
                nc.vector.tensor_tensor(bc_parts[q][low, :], bc_rest[low, :], bc_mid[low, :],
                                        ALU.subtract).then_inc(f_split, 1)

            def one_plus_exp(b):
                v.wait_ge(f_zexp, b + 1)
                nc.vector.tensor_scalar(zcor[:, :, :], zexp[:, :, :], 1.0, -1.0, ALU.add,
                                        ALU.add).then_inc(f_cor, 1)

            def make_delta(b, q):
                v.wait_ge(f_miss, b + 1)
                v.wait_ge(z_chain, b + 1)
                nc.vector.tensor_tensor(delta[q][:, :, :], z[:, :, :], zmiss[:, :, :], ALU.add).then_inc(f_delta, 1)

            def add_log(b):
                v.wait_ge(f_zln, b + 1)
                nc.vector.scalar_tensor_tensor(z[:, :, :], z[:, :, :], 0.0, zln[:, :, :],
                                               ALU.max, ALU.add).then_inc(z_chain, 1)

            def make_dx(b, q):
                v.wait_ge(f_delta, b + 1)
                v.wait_ge(f_u, (b + 1) * (EC + 1))
                nc.vector.tensor_tensor(dx[q][:, :, :], delta[q][:, :, :], u[q][:, :, :],
                                        ALU.mult).then_inc(f_dx, 1)

            def scan(b, q, with_entry, with_front, with_tail):
                for n in range(NS):
                    k = b * NS + n
                    if n == 4 and with_tail:
                        residual(b - 1)
                    if n == 6 and with_tail:
                        normalize(b - 1)
                    v.wait_ge(s_decay, made(k))
                    v.wait_ge(s_inject, made(k))
                    nc.vector.tensor_tensor_scan(
                        h[:, n % 2, :, :].rearrange("p c t -> p (c t)"),
                        decay[:, n % RING, :, :].rearrange("p c t -> p (c t)"),
                        inject[:, n % RING, :, :].rearrange("p c t -> p (c t)"),
                        0.0, ALU.mult, ALU.add).then_inc(s_h, 1)
                    if n == 0 and with_tail:
                        gate(b - 1, 1 - q)
                    v.wait_ge(s_h, made(k))
                    v.wait_ge(s_bc_all, made(k))
                    v.wait_ge(s_sum, free(k, 2))
                    nc.vector.tensor_tensor(
                        hc[:, n % 2, :, :], h[:, n % 2, :, :],
                        bc_all[:, n % RING, 1:2, :].to_broadcast([P, EC, L]), ALU.mult).then_inc(s_hc, 1)
                    if with_front and n == 9:
                        split_bc(b + 1, 1 - q)
                    if with_front and n == 10:
                        take_z(b + 1)
                    if with_front and n == 11:
                        one_plus_exp(b + 1)
                    if with_front and n == 12:
                        add_log(b + 1)
                    if with_front and n == 13:
                        make_delta(b + 1, 1 - q)
                        make_dx(b + 1, 1 - q)

            def gate(b, q):
                v.wait_ge(y_done, b + 1)
                v.sem_inc(s_sum, 1)
                nc.vector.tensor_tensor(y_gated[:, :, :], ps_y[:, :, :], skip[q][:, :, :],
                                        ALU.mult).then_inc(y_gated_done, 1)

            def residual(b):
                v.wait_ge(out_done, b + 1)
                chain = Chain(v, d_chain, b * 6, 3)
                x_b = X[:, bass.ds(b * TT, TT), :]
                chain.link(nc.vector.scalar_tensor_tensor(
                    res[:, :, :], x_b, 2.0, ps_misc[:, :].rearrange("p (s d) -> p s d", s=TT),
                    ALU.mult, ALU.add))
                v.sem_inc(res_free, 1)
                for s in range(TT):
                    last = nc.vector.bn_stats(stats[:, s, :], res[:, s, :])
                chain.link(last)
                v.sem_inc(settled, 1)
                for s in range(TT):
                    last = nc.vector.bn_aggr(mv[:, s, :], stats[:, s, :])
                chain.link(last)
                chain.close()
                nc.vector.tensor_scalar(var[:, :], mv[:, :, 1], EPS, None, ALU.add).then_inc(var_made, 1)

            def normalize(b):
                v.wait_ge(r0_made, b + 1)
                chain = Chain(v, d_chain, b * 6 + 3, 3)
                chain.link(nc.vector.tensor_tensor(r1[:, :], r0[:, :], r0[:, :], ALU.mult))
                chain.link(nc.vector.tensor_tensor(r1[:, :], r1[:, :], var[:, :], ALU.mult))
                chain.link(nc.vector.tensor_scalar(r1[:, :], r1[:, :], -0.5, 1.5, ALU.mult, ALU.add))
                chain.close()
                nc.vector.tensor_tensor(r2[:, :], r1[:, :], r0[:, :], ALU.mult).then_inc(x_made, 1)
                v.wait_ge(x_made, b * 2 + 1)
                for s in range(TT):
                    last = nc.vector.tensor_scalar(X[:, bass.ds(b * TT + s, 1), :], res[:, s, :],
                                                   mv[:, s, 0:1], r2[:, s:s + 1], ALU.subtract, ALU.mult)
                last.then_inc(x_made, 1)

            split_bc(0, 0)
            take_z(0)
            one_plus_exp(0)
            add_log(0)
            make_delta(0, 0)
            make_dx(0, 0)
            refine(REST, 1)
            steps(v, scan)
            gate(B - 1, 1)
            residual(B - 1)
            normalize(B - 1)
            v.wait_ge(x_made, 2 * B)

        @block.tensor
        def _(pe):
            pe.sem_inc(s_sum, RING)

            def transposes(b):
                pe.wait_ge(f_xn, b + 1)
                for c in range(DC):
                    for s in range(TT):
                        last = nc.tensor.transpose(ps_tr[:, c, s * P:(s + 1) * P],
                                                   xn[:, s, c * P:(c + 1) * P], ident[:, :])
                last.then_inc(f_tr, 1)

            def project(w, chunks, done):
                for c in chunks:
                    for k in range(DC):
                        last = nc.tensor.matmul(ps_pr[:, c, :], w[:, k, c * P:(c + 1) * P], xnT[:, k, :],
                                                start=(k == 0), stop=(k == DC - 1))
                    if c % 2 == 1:
                        last.then_inc(done, 1)

            def project_in(b, chunks):
                if chunks[0] == 0:
                    pe.wait_ge(f_xnT, b + 1)
                for c in chunks:
                    if c % 2 == 0 and not (isinstance(b, int) and b == 0):
                        pe.wait_ge(f_u, (b - 1) * (EC + 1) + c + 2)
                    project(w_in, (c,), f_in)

            def project_skip(b, chunks):
                for c in chunks:
                    if c % 2 == 0:
                        pe.wait_ge(f_xin, b * 2 + c // 2 + 1)
                        if c == 0 and not (isinstance(b, int) and b == 0):
                            pe.wait_ge(f_zsb, b)
                    project(w_skip, (c,), f_skip)

            def conv(b, chunks):
                for c in chunks:
                    if c % 2 == 0:
                        pe.wait_ge(f_skip_raw, b * 2 + c // 2 + 1)
                    for k in range(TAPS):
                        last = nc.tensor.matmul(ps_pr[:, c, :], conv_diag[:, c, k, :], xin[:, c, k:k + L],
                                                start=(k == 0), stop=(k == TAPS - 1))
                    if c % 2 == 1:
                        last.then_inc(f_conv, 1)

            def project_u(b, q, at, n, col):
                for k in range(EC):
                    last = nc.tensor.matmul(ps_misc[0:n, col:col + L], w_dbc[:, k, at:at + n], u[q][:, k, :],
                                            start=(k == 0), stop=(k == EC - 1))
                return last

            def delta_low(b, q):
                pe.wait_ge(f_u, b * (EC + 1) + EC)
                project_u(b, q, 0, DD, 0)

            def rows_b_c(b, q):
                project_u(b, q, DD, PARTS * NBC, L).then_inc(f_dbc, 1)

            def delta_up(b, q, with_entry):
                pe.wait_ge(f_dbc_sb, b + 1)
                if with_entry:
                    pe.wait_ge(f_xin, b * 2 + 4)
                for c in range(EC):
                    last = nc.tensor.matmul(ps_pr[:, c, :], w_d2[:, c * P:(c + 1) * P], dlow[:, :],
                                            start=True, stop=True)
                last.then_inc(f_z, 1)

            def spread(b, q, n):
                if n == 0:
                    pe.wait_ge(f_split, b + 1)
                k = b * NS + n
                pe.wait_ge(s_bc_all, free(k, 2))
                for j in range(2):
                    at = j * NS + n
                    last = nc.tensor.matmul(ps_bc[n % 2][:, j, :],
                                            pick[:, at:at + 1].to_broadcast([PARTS * NBC, P]),
                                            bc_parts[q][:, :], start=True, stop=True)
                last.then_inc(s_bc, 1)

            def add_state(b, n):
                k = b * NS + n
                if n == 0:
                    pe.wait_ge(y_gated_done, b + 1)
                pe.wait_ge(s_hc, made(k))
                for c in range(0, EC, 2):
                    last = nc.tensor.matmul(ps_y[:, c:c + 2, :], ident[:, :], hc[:, n % 2, c:c + 2, :],
                                            start=(n == 0), stop=(n == NS - 1))
                last.then_inc(s_sum if n < NS - 1 else y_done, 1)

            def add_input(b, q):
                for c in range(EC):
                    nc.tensor.matmul(ps_y[:, c, :], d_diag[:, c, :], u[q][:, c, :],
                                     start=False, stop=False, skip_group_check=True)

            def scan(b, q, with_entry, with_front, with_tail):
                for n in range(NS):
                    ahead(spread, b, q, n, with_front)
                    if with_front and n == 0:
                        conv(b + 1, (0,))
                    if with_tail and n in (1, 2):
                        project_out(b - 1, n - 1)
                    if with_entry and n == 3:
                        transposes(b + 2)
                    if with_front and n in (3, 4, 5):
                        conv(b + 1, (n - 2,))
                    if with_entry and n == 6:
                        project_in(b + 2, (0, 1))
                    if with_front and n == 7:
                        if with_tail:
                            pe.wait_ge(res_free, b)
                        delta_low(b + 1, 1 - q)
                    if with_front and n == 8:
                        rows_b_c(b + 1, 1 - q)
                    if with_entry and n == 8:
                        project_in(b + 2, (2, 3))
                    if with_front and n == 9:
                        delta_up(b + 1, 1 - q, with_entry)
                    if with_entry and n == 11:
                        project_skip(b + 2, (0, 1))
                    if with_entry and n == 12:
                        project_skip(b + 2, (2, 3))
                    add_state(b, n)
                    if n == 0:
                        add_input(b, q)

            def project_out(b, s):
                if s == 0:
                    pe.wait_ge(y_gated_done, b + 2)
                for k in range(EC):
                    last = nc.tensor.matmul(ps_misc[:, s * D:(s + 1) * D],
                                            y_gated[:, k, s * P:(s + 1) * P], w_out[:, k, :],
                                            start=(k == 0), stop=(k == EC - 1))
                if s == TT - 1:
                    last.then_inc(out_done, 1)

            transposes(0)
            pe.wait_ge(w_first, 16 * 2)
            project_in(0, range(EC))
            pe.wait_ge(w_loaded, 16 * W_LATER)
            project_skip(0, range(EC))
            pe.wait_ge(diag_made, 1)
            pe.wait_ge(pads_zero, 2)
            conv(0, range(EC))
            delta_low(0, 0)
            rows_b_c(0, 0)
            transposes(1)
            project_in(1, range(EC))
            delta_up(0, 0, True)
            for n in range(LEAD):
                spread(0, 0, n)
            project_skip(1, range(EC))
            steps(pe, scan)
            for s in range(TT):
                project_out(B - 1, s)


class FfnWeights:

    def __init__(self, nc, ctx):
        def sb(name, shape, dt=F32):
            return ctx.enter_context(nc.sbuf_tensor(name, shape, dt))

        self.up = sb("s_up", [P, DC, 2 * FS])
        self.down = sb("s_down", [P, FSC, D])
        self.b_up = sb("s_b_up", [P, 2 * FSC])
        self.b_down = sb("s_b_down", [P, D])
        self.factor = sb("s_factor", [P, FSC])
        self.router = sb("router", [P, DC, NE])
        self.e_down = sb("e_down", [P, NE, FEC, D])
        self.e_factor = sb("e_factor", [P, NE, FEC])
        self.bias = sb("e_bias", [P, NBP])
        self.rest = sb("e_rest", [P, NBP])
        self.part = sb("e_part", [P, PARTS, NBP], BF16)
        self.rows = sb("e_rows", [PARTS, NE, NB], BF16)
        self.zero = sb("zero", [P, D])


def attention_phase(nc, dram, X, ident, ffn, logits, slots_dram):
    with ExitStack() as ctx:
        def sb(name, shape, dt=F32):
            return ctx.enter_context(nc.sbuf_tensor(name, shape, dt))

        def ps(name, shape, dt=F32):
            return ctx.enter_context(nc.psum_tensor(name, shape, dt))

        def sem(name):
            return ctx.enter_context(nc.semaphore(name))

        wq, wk, wv = (sb(n, [P, DC, D]) for n in ("wq", "wk", "wv"))
        wo = sb("wo", [P, HG, D])
        bq, bk = sb("bq", [P, DC]), sb("bk", [P, DC])
        head_rows = sb("head_rows", [P, HC])
        bv, bo = sb("bv", [P, D]), sb("bo", [P, D])
        cos, sin = sb("cos", [P, DC, L]), sb("sin", [P, DC, L])
        ctxT = [sb(f"ctxT{j}", [P, DC, L]) for j in range(2)]
        xs = sb("xs", [P, TT, D])
        rope_a, rope_b, qr = (sb(n, [P, DC, L]) for n in ("rope_a", "rope_b", "qr"))
        krope_a, krope_b = sb("krope_a", [P, DC, L]), sb("krope_b", [P, DC, L])
        kr = sb("kr", [P, DC, L])
        QT = [sb(f"QT{j}", [P, DC, L]) for j in range(2)]
        kb = sb("kb", [P, DC, L])
        KT = sb("KT", [P, DC, HC, L])
        V = [sb(f"V{j}", [P, TT, NH, 32]) for j in range(2)]
        neg_max = sb("neg_max", [P, 2, TT])
        prob = sb("prob", [P, 2, TT, L])
        total = sb("total", [P, 2, TT])
        inv = sb("inv", [P, 2, TT])
        probT = sb("probT", [P, 2 * HG, TT, L])
        oT = sb("oT", [P, HG, L])
        x2 = sb("x2", [P, TT, D])
        x2T = sb("x2T", [P, DC, L])
        res = sb("a_res", [P, TT, D])
        stats, mv, var = sb("a_stats", [P, TT, 6]), sb("a_mv", [P, TT, 2]), sb("a_var", [P, TT])
        ln_var, r0, r1, r2 = (sb(n, [P, TT]) for n in ("a_ln_var", "a_r0", "a_r1", "a_r2"))

        ps_m0 = ps("ps_m0", [P, 2, 256])
        ps_m1 = ps("ps_m1", [P, 2, 256])
        ps_s = [ps(f"ps_s{j}", [P, TT, L]) for j in range(2)]
        ps_t = [ps(f"ps_t{j}", [P, TT, L]) for j in range(2)]
        ps_o = ps("ps_o", [P, HG, L])

        w_got, v_zero, bq_scaled = sem("w_got"), sem("v_zero"), sem("bq_scaled")
        ctx_in = [sem(f"ctx_in{j}") for j in range(2)]
        f_xs, f_tr, f_qr, f_kr, f_q, f_qs, f_k, f_ks, f_v, f_vs = (
            sem("af_" + n) for n in ("xs", "tr", "qr", "kr", "q", "qs", "k", "ks", "v", "vs"))
        q_chain, k_chain, n_chain = sem("q_chain"), sem("k_chain"), sem("n_chain")
        h_s, h_max, h_exp, h_inv, h_norm, h_t, h_pt, h_pv = (
            sem("h_" + n) for n in ("s", "max", "exp", "inv", "norm", "t", "pt", "pv"))
        t_o, t_w, t_res, t_var, t_lnv, t_r0, t_x, t_settled = (
            sem("t_" + n) for n in ("o", "w", "res", "var", "lnv", "r0", "x", "settled"))
        f_heads = sem("f_heads")
        l_x, l_tr, l_xT, l_l, l_got = (sem("l_" + n) for n in ("x", "tr", "xT", "l", "got"))
        ffn_in, down_in = sem("ffn_in"), sem("down_in")
        scaled, b_chain, rows_moved, zero_made, zeroed = (
            sem("ffn_" + n) for n in ("scaled", "b_chain", "rows_moved", "zero_made", "zeroed"))
        rows_dram = nc.dram_tensor("bias_rows", (PARTS, P, NBP), BF16, kind="Internal").ap()
        block = ctx.enter_context(nc.Block())

        def made(k):
            return k + 1 + 2

        def free(k):
            return k + 1

        loads = ((wq[:, :, :], dram["WqT"].rearrange("(c p) e -> p c e", p=P)),
                 (wk[:, :, :], dram["WkT"].rearrange("(c p) e -> p c e", p=P)),
                 (wv[:, :, :], dram["WvT"].rearrange("(c p) e -> p c e", p=P)),
                 (wo[:, :, :], dram["WoT"].rearrange("(c p) e -> p c e", p=P)),
                 (bq[:, :], dram["bq"]), (bk[:, :], dram["bk"]),
                 (head_rows[:, :], dram["head_rows"]),
                 (bv[:, :], dram["bv"].to_broadcast([P, D])), (bo[:, :], dram["bo"].to_broadcast([P, D])),
                 (cos[:, :, :], dram["cosT"].rearrange("(c p) t -> p c t", p=P)),
                 (sin[:, :, :], dram["sinT"].rearrange("(c p) t -> p c t", p=P)))

        def steps(eng, body):
            body(0, 0, True, False)
            with eng.Fori(0, B // 2 - 1) as i:
                body(i * 2 + 1, 1, True, True)
                body(i * 2 + 2, 0, True, True)
            body(B - 1, 1, False, True)

        @block.sync
        def _(sp):
            ctx_v = dram["ctxT"].rearrange("b (c p) t -> p b c t", p=P)

            def load_ctx(b, q):
                sp.dma_start(ctxT[q][:, :, :], ctx_v[:, bass.ds(b, 1), :, :]).then_inc(ctx_in[q], 16)

            load_ctx(0, 0)
            for dst, src in loads:
                sp.dma_start(dst, src).then_inc(w_got, 16)
            load_ctx(1, 1)
            with sp.Fori(0, B // 2 - 1) as i:
                for q in range(2):
                    b = i * 2 + q
                    sp.wait_ge(f_v, b + 1)
                    sp.wait_ge(f_kr, b + 1)
                    load_ctx(b + 2, q)

        ffn_loads = ((ffn.up[:, :, :], dram["s_fc1T"].rearrange("(c p) e -> p c e", p=P)),
                     (ffn.b_up[:, :], dram["s_fc1_b"]),
                     (ffn.b_down[:, :], dram["s_fc2_b"].to_broadcast([P, D])),
                     (ffn.router[:, :, :], dram["gateT"].rearrange("(c p) e -> p c e", p=P)))
        down_v = dram["fc2T"].rearrange("e (c p) f -> p e c f", p=P)
        down_loads = ((ffn.bias[:, :], dram["e_bias"]), (ffn.factor[:, :], dram["s_mult"]), (ffn.e_factor[:, :, :], dram["e_mult"]),
                      (ffn.down[:, :, :], dram["s_fc2T"].rearrange("(c p) e -> p c e", p=P)),
                      *((ffn.e_down[:, e, :, :], down_v[:, e, :, :]) for e in range(NE)))

        @block.gpsimd
        def _(g):
            nc.gpsimd.memset(ffn.zero[:, :], 0.0).then_inc(zero_made, 1)
            for q in range(2):
                nc.gpsimd.memset(V[q][:, :, :, :], 0.0).then_inc(v_zero, 1)

            def head_keys(b):
                g.wait_ge(f_ks, b + 1)
                for c in range(DC):
                    if not (isinstance(b, int) and b == 0):
                        g.wait_ge(h_s, (b - 1) * NH + (c + 1) * HC)
                    nc.gpsimd.tensor_tensor(KT[:, c, :, :], kb[:, c, :].unsqueeze(1).to_broadcast([P, HC, L]),
                                            head_rows[:, :].unsqueeze(2).to_broadcast([P, HC, L]),
                                            ALU.mult).then_inc(f_heads, 1)

            def front(b, q, loads_before):
                g.wait_ge(ctx_in[q], loads_before * 16 + 16)
                chain = Chain(g, k_chain, b * 2, 2)
                nc.gpsimd.tensor_tensor(krope_a[:, :, :], ctxT[q][:, :, :], cos[:, :, :], ALU.mult)
                for c in range(DC):
                    last = nc.gpsimd.tensor_tensor(krope_b[:, c, :], ctxT[q][:, 1 - c, :], sin[:, c, :],
                                                   ALU.mult)
                chain.link(last)
                if not (isinstance(b, int) and b == 0):
                    g.wait_ge(f_k, b)
                chain.link(nc.gpsimd.tensor_tensor(kr[:, :, :], krope_a[:, :, :], krope_b[:, :, :], ALU.add))
                chain.close()
                g.sem_inc(f_kr, 1)

            g.wait_ge(w_got, 16 * len(loads))
            front(0, 0, 0)
            head_keys(0)
            front(1, 1, 0)
            with g.Fori(0, B // 2 - 1) as i:
                head_keys(i * 2 + 1)
                front(i * 2 + 2, 0, i + 1)
                head_keys(i * 2 + 2)
                front(i * 2 + 3, 1, i + 1)
            head_keys(B - 1)

            g.wait_ge(down_in, 16 * len(down_loads))
            nc.gpsimd.tensor_tensor(ffn.down[:, :, :], ffn.down[:, :, :],
                                    ffn.factor[:, :].unsqueeze(2).to_broadcast([P, FSC, D]),
                                    ALU.mult).then_inc(scaled, 1)
            e_down = ffn.e_down[:, :, :, :].rearrange("p e c f -> p (e c) f")
            nc.gpsimd.tensor_tensor(
                e_down, e_down,
                ffn.e_factor[:, :, :].rearrange("p e c -> p (e c)").unsqueeze(2).to_broadcast([P, NE * FEC, D]),
                ALU.mult).then_inc(scaled, 1)
            bias, rest, part = ffn.bias, ffn.rest, ffn.part
            chain = Chain(g, b_chain, 0, 5)
            chain.link(nc.gpsimd.tensor_copy(part[:, 0, :], bias[:, :]))
            chain.link(nc.gpsimd.tensor_tensor(rest[:, :], bias[:, :], part[:, 0, :], ALU.subtract))
            chain.link(nc.gpsimd.tensor_copy(part[:, 1, :], rest[:, :]))
            chain.link(nc.gpsimd.tensor_tensor(rest[:, :], rest[:, :], part[:, 1, :], ALU.subtract))
            chain.link(nc.gpsimd.tensor_copy(part[:, 2, :], rest[:, :]))
            chain.close()
            g.dma_start(rows_dram.rearrange("r p n -> p r n"), part[:, :, :]).then_inc(rows_moved, 16)
            g.wait_ge(rows_moved, 16)
            g.dma_start(ffn.rows[:, :, :].rearrange("r e n -> r (e n)"),
                        rows_dram.rearrange("r p n -> r (p n)")).then_inc(rows_moved, 16)
            g.wait_ge(rows_moved, 32)
            g.wait_ge(scaled, 2)
            g.wait_ge(zeroed, 16)

        @block.scalar
        def _(act):
            act.sem_inc(h_exp, 2)
            act.sem_inc(h_pt, 2)
            act.preload_act_table_set(EXP_LN)

            def copy_x(b):
                nc.scalar.activation(xs[:, :, :], X[:, bass.ds(b * TT, TT), :], ACT.Copy).then_inc(f_xs, 1)

            def take_q(b, q):
                act.wait_ge(f_q, b + 1)
                for c in range(DC):
                    last = nc.scalar.activation(QT[q][:, c, :], ps_m1[:, c, :], ACT.Identity,
                                                bias=bq[:, c:c + 1], scale=SCALE)
                last.then_inc(f_qs, 1)

            def exps(k, j):
                act.wait_ge(h_max, k + 1)
                act.wait_ge(h_t, free(k))
                for s in range(TT):
                    last = nc.scalar.activation(prob[:, j, s, :], ps_s[j][:, s, :], ACT.Exp,
                                                bias=neg_max[:, j, s:s + 1], accum_out=total[:, j, s:s + 1])
                last.then_inc(h_exp, 1)

            def take_t(k, G, h):
                act.wait_ge(h_t, made(k))
                if h % HG == 0:
                    act.wait_ge(h_pv, free(G))
                nc.scalar.activation(probT[:, h % (2 * HG), :, :], ps_t[h % 2][:, :, :],
                                     ACT.Copy).then_inc(h_pt, 1)

            def heads(b, q, with_front, with_tail):
                for h in range(NH):
                    k = b * NH + h
                    if h < NH - 1 or with_front:
                        exps(k + 1, (h + 1) % 2)
                    take_t(k, b * (NH // HG) + h // HG, h)
                    if with_front and h == 0:
                        copy_x(b + 1)
                    if with_tail and h == 1:
                        tail_o(b - 1)
                    if with_tail and h == 6:
                        tail_root(b - 1)
                    if with_front and h == 7:
                        take_q(b + 1, 1 - q)
                    if with_tail and h == 9:
                        copy_x2(b - 1)
                    if with_tail and h == 12:
                        take_x2T(b - 1)
                    if with_tail and h == 14:
                        take_logits(b - 1)

            def copy_x2(b):
                act.wait_ge(t_x, b * 2 + 2)
                nc.scalar.activation(x2[:, :, :], X[:, bass.ds(b * TT, TT), :], ACT.Copy).then_inc(l_x, 1)

            def take_x2T(b):
                act.wait_ge(l_tr, b + 1)
                nc.scalar.activation(x2T[:, :, :], ps_m0[:, :, :], ACT.Copy).then_inc(l_xT, 1)

            def take_logits(b):
                act.wait_ge(l_l, b + 1)
                nc.scalar.activation(logits[:, bass.ds(b * TT, TT), 0:NE], ps_m1[:, :, 0:NE],
                                     ACT.Copy).then_inc(l_got, 1)

            def tail_o(b):
                act.wait_ge(h_pv, made(b * (NH // HG) + NH // HG - 1))
                nc.scalar.activation(oT[:, :, :], ps_o[:, :, :], ACT.Copy).then_inc(t_o, 1)

            def tail_root(b):
                act.wait_ge(t_var, b + 1)
                nc.scalar.activation(ln_var[:, :], var[:, :], ACT.Ln).then_inc(t_lnv, 1)
                act.wait_ge(t_lnv, b + 1)
                nc.scalar.activation(r0[:, :], ln_var[:, :], ACT.Exp, scale=-0.5).then_inc(t_r0, 1)

            act.wait_ge(w_got, 16 * len(loads))
            copy_x(0)
            for dst, src in ffn_loads:
                act.dma_start(dst, src).then_inc(ffn_in, 16)
            for dst, src in down_loads:
                act.dma_start(dst, src).then_inc(down_in, 16)
            act.wait_ge(zero_made, 1)
            act.dma_start(slots_dram.rearrange("(i p) d -> p i d", p=P),
                          ffn.zero[:, :].unsqueeze(1).to_broadcast([P, SLOT_TILES, D])).then_inc(zeroed, 16)
            act.wait_ge(bq_scaled, 1)
            take_q(0, 0)
            exps(0, 0)
            steps(act, heads)
            tail_o(B - 1)
            tail_root(B - 1)
            copy_x2(B - 1)
            take_x2T(B - 1)
            take_logits(B - 1)
            act.wait_ge(l_got, B)

        @block.vector
        def _(v):
            v.wait_ge(w_got, 16 * len(loads))
            nc.vector.tensor_scalar(bq[:, :], bq[:, :], SCALE, None, ALU.mult).then_inc(bq_scaled, 1)

            def rope_q(b):
                v.wait_ge(f_tr, b + 1)
                chain = Chain(v, q_chain, b, 1)
                nc.vector.tensor_tensor(rope_a[:, :, :], ps_m0[:, :, :], cos[:, :, :], ALU.mult)
                for c in range(DC):
                    last = nc.vector.tensor_tensor(rope_b[:, c, :], ps_m0[:, 1 - c, :], sin[:, c, :], ALU.mult)
                chain.link(last)
                nc.vector.tensor_tensor(qr[:, :, :], rope_a[:, :, :], rope_b[:, :, :], ALU.add).then_inc(f_qr, 1)

            def take_k(b):
                v.wait_ge(f_k, b + 1)
                if not (isinstance(b, int) and b == 0):
                    v.wait_ge(f_heads, b * DC)
                for c in range(DC):
                    last = nc.vector.tensor_scalar(kb[:, c, :], ps_m0[:, c, :], bk[:, c:c + 1], None, ALU.add)
                last.then_inc(f_ks, 1)

            def take_v(b, q):
                v.wait_ge(f_v, b + 1)
                for s in range(TT):
                    last = nc.vector.tensor_tensor(
                        V[q][:, s, :, 0:DK], ps_m1[:, s, :].rearrange("p (h d) -> p h d", h=NH),
                        bv[:, :].rearrange("p (h d) -> p h d", h=NH), ALU.add)
                last.then_inc(f_vs, 1)

            def row_max(k, j):
                v.wait_ge(h_s, k + 1)
                nc.vector.tensor_reduce(neg_max[:, j, :], ps_s[j][:, :, :], AXX, ALU.max,
                                        negate=True).then_inc(h_max, 1)

            def normalize(k, j):
                v.wait_ge(h_exp, made(k))
                nc.vector.reciprocal(inv[:, j, :], total[:, j, :]).then_inc(h_inv, 1)
                v.wait_ge(h_inv, k + 1)
                for s in range(TT):
                    last = nc.vector.tensor_scalar(prob[:, j, s, :], prob[:, j, s, :], inv[:, j, s:s + 1],
                                                   None, ALU.mult)
                last.then_inc(h_norm, 1)

            def tail_res(b):
                v.wait_ge(t_w, b + 1)
                chain = Chain(v, n_chain, b * 6, 1)
                chain.link(nc.vector.tensor_tensor(res[:, :, :], X[:, bass.ds(b * TT, TT), :], ps_m0[:, :, :],
                                                   ALU.add))
                v.sem_inc(t_res, 1)
                chain.close()
                nc.vector.tensor_tensor(res[:, :, :], res[:, :, :],
                                        bo[:, :].unsqueeze(1).to_broadcast([P, TT, D]),
                                        ALU.add).then_inc(n_chain, 1)

            def tail_stats(b):
                v.wait_ge(n_chain, b * 6 + 2)
                chain = Chain(v, n_chain, b * 6 + 2, 1)
                for s in range(TT):
                    last = nc.vector.bn_stats(stats[:, s, :], res[:, s, :])
                chain.link(last)
                v.sem_inc(t_settled, 1)
                for s in range(TT):
                    last = nc.vector.bn_aggr(mv[:, s, :], stats[:, s, :])
                last.then_inc(t_settled, 1)
                v.wait_ge(t_settled, b * 2 + 2)
                nc.vector.tensor_scalar(var[:, :], mv[:, :, 1], EPS, None, ALU.add).then_inc(t_var, 1)

            def tail_norm(b):
                v.wait_ge(t_r0, b + 1)
                chain = Chain(v, n_chain, b * 6 + 3, 3)
                chain.link(nc.vector.tensor_tensor(r1[:, :], r0[:, :], r0[:, :], ALU.mult))
                chain.link(nc.vector.tensor_tensor(r1[:, :], r1[:, :], var[:, :], ALU.mult))
                chain.link(nc.vector.tensor_scalar(r1[:, :], r1[:, :], -0.5, 1.5, ALU.mult, ALU.add))
                nc.vector.tensor_tensor(r2[:, :], r1[:, :], r0[:, :], ALU.mult).then_inc(t_x, 1)
                v.wait_ge(t_x, b * 2 + 1)
                for s in range(TT):
                    last = nc.vector.tensor_scalar(X[:, bass.ds(b * TT + s, 1), :], res[:, s, :],
                                                   mv[:, s, 0:1], r2[:, s:s + 1], ALU.subtract, ALU.mult)
                last.then_inc(t_x, 1)

            def heads(b, q, with_front, with_tail):
                for h in range(NH):
                    k = b * NH + h
                    normalize(k, h % 2)
                    if h < NH - 2 or with_front:
                        row_max(k + 2, h % 2)
                    if with_front and h == 1:
                        rope_q(b + 1)
                    if with_tail and h == 4:
                        tail_res(b - 1)
                    if with_tail and h == 5:
                        tail_stats(b - 1)
                    if with_tail and h == 7:
                        tail_norm(b - 1)
                    if with_front and h == 9:
                        take_k(b + 1)
                    if with_front and h == 11:
                        take_v(b + 1, 1 - q)

            rope_q(0)
            take_k(0)
            v.wait_ge(v_zero, 2)
            take_v(0, 0)
            row_max(0, 0)
            row_max(1, 1)
            steps(v, heads)
            tail_res(B - 1)
            tail_stats(B - 1)
            tail_norm(B - 1)
            v.wait_ge(t_x, 2 * B)

        @block.tensor
        def _(pe):
            pe.sem_inc(h_t, 2)
            pe.sem_inc(h_pv, 2)

            def transposes(b):
                pe.wait_ge(f_xs, b + 1)
                for c in range(DC):
                    for s in range(TT):
                        last = nc.tensor.transpose(ps_m0[:, c, s * P:(s + 1) * P],
                                                   xs[:, s, c * P:(c + 1) * P], ident[:, :])
                last.then_inc(f_tr, 1)

            def project(dst, w, src, done, c):
                for k in range(DC):
                    last = nc.tensor.matmul(dst[:, c, :], w[:, k, c * P:(c + 1) * P], src[:, k, :],
                                            start=(k == 0), stop=(k == DC - 1))
                if c == DC - 1:
                    last.then_inc(done, 1)

            def values(q, s):
                for k in range(DC):
                    last = nc.tensor.matmul(ps_m1[:, s, :], ctxT[q][:, k, s * P:(s + 1) * P], wv[:, k, :],
                                            start=(k == 0), stop=(k == DC - 1))
                if s == TT - 1:
                    last.then_inc(f_v, 1)

            def scores(b, h, q):
                c, j = divmod(h, HC)
                if j == 0:
                    pe.wait_ge(f_heads, b * DC + c + 1)
                pe.wait_ge(h_exp, free(b * NH + h))
                for s in range(TT):
                    last = nc.tensor.matmul(ps_s[h % 2][:, s, :], QT[q][:, c, s * P:(s + 1) * P],
                                            KT[:, c, j, :], start=True, stop=True)
                last.then_inc(h_s, 1)

            def turn(k, h):
                pe.wait_ge(h_norm, k + 1)
                pe.wait_ge(h_pt, free(k))
                for t in range(TT):
                    for s in range(TT):
                        last = nc.tensor.transpose(ps_t[h % 2][:, t, s * P:(s + 1) * P],
                                                   prob[:, h % 2, s, t * P:(t + 1) * P], ident[:, :])
                last.then_inc(h_t, 1)

            def weigh(b, g, q, fresh):
                if g == 0 and fresh:
                    pe.wait_ge(t_o, b)
                pe.wait_ge(h_pt, made(b * NH + g * HG + HG - 1))
                for t in range(TT):
                    for j in range(HG):
                        h = g * HG + j
                        last = nc.tensor.matmul(ps_o[32 * j:32 * j + 32, g, :], V[q][:, t, h, :],
                                                probT[:, h % (2 * HG), t, :],
                                                start=(t == 0), stop=(t == TT - 1))
                last.then_inc(h_pv, 1)

            def project_out(b, s):
                if s == 0:
                    pe.wait_ge(t_o, b + 1)
                for g in range(HG):
                    last = nc.tensor.matmul(ps_m0[:, s, :], oT[:, g, s * P:(s + 1) * P], wo[:, g, :],
                                            start=(g == 0), stop=(g == HG - 1))
                if s == TT - 1:
                    last.then_inc(t_w, 1)

            def heads(b, q, with_front, with_tail):
                for h in range(NH):
                    k = b * NH + h
                    if h < NH - 2:
                        scores(b, h + 2, q)
                    elif with_front:
                        scores(b + 1, h + 2 - NH, 1 - q)
                    if h % HG == 0 and h > 0:
                        weigh(b, h // HG - 1, q, with_tail)
                    if h == 0 and with_tail:
                        weigh(b - 1, NH // HG - 1, 1 - q, True)
                    turn(k, h)
                    if with_front and h == 1:
                        transposes(b + 1)
                    if with_tail and h in (2, 3):
                        if with_front:
                            pe.wait_ge(f_qr, b + 2)
                        project_out(b - 1, h - 2)
                    if with_front and h in (5, 6):
                        if with_tail and not (isinstance(b, int) and b == 1):
                            pe.wait_ge(l_got, b - 1)
                        pe.wait_ge(f_qr, b + 2)
                        project(ps_m1, wq, qr, f_q, h - 5)
                    if with_front and h in (7, 8):
                        if with_tail:
                            pe.wait_ge(t_res, b)
                        pe.wait_ge(f_kr, b + 2)
                        project(ps_m0, wk, kr, f_k, h - 7)
                    if with_front and h in (9, 10):
                        pe.wait_ge(f_qs, b + 2)
                        values(1 - q, h - 9)
                    if with_tail and h == 11:
                        if with_front:
                            pe.wait_ge(f_ks, b + 2)
                        turn_x2(b - 1)
                    if with_front and h == 13:
                        pe.wait_ge(f_vs, b + 2)
                    if with_tail and h == 13:
                        route(b - 1)

            def turn_x2(b):
                pe.wait_ge(l_x, b + 1)
                for c in range(DC):
                    for s in range(TT):
                        last = nc.tensor.transpose(ps_m0[:, c, s * P:(s + 1) * P],
                                                   x2[:, s, c * P:(c + 1) * P], ident[:, :])
                last.then_inc(l_tr, 1)

            def route(b):
                pe.wait_ge(l_xT, b + 1)
                for s in range(TT):
                    for k in range(DC):
                        last = nc.tensor.matmul(ps_m1[:, s, 0:NE], x2T[:, k, s * P:(s + 1) * P],
                                                ffn.router[:, k, :], start=(k == 0), stop=(k == DC - 1))
                last.then_inc(l_l, 1)

            pe.wait_ge(w_got, 16 * len(loads))
            transposes(0)
            pe.wait_ge(f_qr, 1)
            pe.wait_ge(f_kr, 1)
            for c in range(DC):
                project(ps_m0, wk, kr, f_k, c)
            for c in range(DC):
                project(ps_m1, wq, qr, f_q, c)
            pe.wait_ge(f_qs, 1)
            for s in range(TT):
                values(0, s)
            pe.wait_ge(f_ks, 1)
            pe.wait_ge(f_vs, 1)
            scores(0, 0, 0)
            scores(0, 1, 0)
            pe.wait_ge(ffn_in, 16 * len(ffn_loads))
            steps(pe, heads)
            weigh(B - 1, NH // HG - 1, 1, True)
            for s in range(TT):
                project_out(B - 1, s)
            pe.wait_ge(t_res, B)
            turn_x2(B - 1)
            pe.wait_ge(l_got, B - 1)
            route(B - 1)


def route_phase(nc, dram, logits, weights, slot_of, expert_of):
    with ExitStack() as ctx:
        def sb(name, shape, dt=F32):
            return ctx.enter_context(nc.sbuf_tensor(name, shape, dt))

        def sem(name):
            return ctx.enter_context(nc.semaphore(name))

        tri, ones = sb("tri", [P, P]), sb("ones", [P, P])
        iota_e = sb("iota_e", [P, NE])
        iota_m = sb("iota_m", [P, NT])
        iota_s = sb("iota_s", [1, SLOT_TILES])
        not_first = sb("not_first", [P, NE, NT])
        top = sb("top", [P, NT, 8])
        top_i = sb("top_i", [P, NT, 8], mybir.dt.uint32)
        top_f = sb("top_f", [P, NT, TOPK])
        shifted = sb("shifted", [P, NT, NE])
        exps = sb("exps", [P, NT, NE])
        top_e = sb("top_e", [P, NT, TOPK])
        total = sb("r_total", [P, NT])
        inv = sb("r_inv", [P, NT])
        top_p = sb("top_p", [P, NT, TOPK])
        hot = sb("hot", [P, TOPK, NT, NE])
        mask = sb("mask", [P, NT, NE])
        before = sb("before", [P, NT, NE])
        tile_sum = sb("tile_sum", [P, NE, NT])
        running = sb("running", [P, NE, NT])
        excl = sb("excl", [P, NE, NT])
        filled = sb("filled", [P, NE, NT])
        n_tiles = sb("n_tiles", [P, NE])
        tile_end = sb("tile_end", [P, NE])
        base = sb("base", [P, NE])
        slot = sb("slot", [P, NT, NE])
        picked = sb("picked", [P, NT, NE])
        slot_f = sb("slot_f", [P, TOPK, NT])
        past = sb("past", [1, SLOT_TILES, NE])
        exp_f = sb("exp_f", [1, SLOT_TILES])
        ps_before = ctx.enter_context(nc.psum_tensor("ps_before", [P, NT, NE], F32))
        ps_total = ctx.enter_context(nc.psum_tensor("ps_total", [P, NT, NE], F32))
        got, top_made, shift_made, exp_made, top_exp, mask_made, counted = (
            sem("r_" + n) for n in ("got", "top", "shift", "exp", "top_exp", "mask", "counted"))
        own, chain_s = sem("r_own"), sem("r_chain")
        block = ctx.enter_context(nc.Block())
        loads = ((tri[:, :], dram["tri"]), (ones[:, :], dram["ones"]),
                 (iota_e[:, :], dram["iota"][0:1, 0:NE].to_broadcast([P, NE])),
                 (iota_m[:, :], dram["iota_m"].to_broadcast([P, NT])),
                 (iota_s[:, :], dram["iota"][0:1, 0:SLOT_TILES]),
                 (not_first[:, :, :].rearrange("p e t -> p (e t)"),
                  dram["not_first"].to_broadcast([P, NE * NT])))

        @block.sync
        def _(sp):
            for dst, src in loads:
                sp.dma_start(dst, src).then_inc(got, 16)

        @block.scalar
        def _(act):
            act.wait_ge(shift_made, 1)
            nc.scalar.activation(exps[:, :, :], shifted[:, :, :], ACT.Exp).then_inc(exp_made, 1)
            act.wait_ge(exp_made, 1)
            nc.scalar.activation(top_e[:, :, :], top_f[:, :, :], ACT.Exp).then_inc(top_exp, 1)

        @block.tensor
        def _(pe):
            pe.wait_ge(mask_made, 1)
            pe.wait_ge(got, 16 * len(loads))
            nc.tensor.matmul(ps_before[:, :, :], tri[:, :], mask[:, :, :], start=True, stop=True)
            nc.tensor.matmul(ps_total[:, :, :], ones[:, :], mask[:, :, :], start=True,
                             stop=True).then_inc(counted, 1)

        @block.vector
        def _(v):
            def by_token(a):
                return a.unsqueeze(2).to_broadcast([P, NT, NE])

            for t in range(NT):
                last = nc.vector.max(top[:, t, :], logits[:, t, 0:NE])
            last.then_inc(top_made, 1)
            v.wait_ge(top_made, 1)
            for t in range(NT):
                last = nc.vector.max_index(top_i[:, t, :], top[:, t, :], logits[:, t, 0:NE])
            nc.vector.tensor_tensor(top_f[:, :, :], top[:, :, 0:TOPK],
                                    top[:, :, 0:1].to_broadcast([P, NT, TOPK]), ALU.subtract)
            nc.vector.tensor_tensor(shifted[:, :, :], logits[:, :, 0:NE], top[:, :, 0:1].to_broadcast([P, NT, NE]),
                                    ALU.subtract).then_inc(shift_made, 1)
            chain = Chain(v, chain_s, 0, 26)
            v.wait_ge(top_exp, 1)
            chain.link(nc.vector.tensor_reduce(total[:, :], exps[:, :, :], AXX, ALU.add))
            chain.link(nc.vector.reciprocal(inv[:, :], total[:, :]))
            chain.link(nc.vector.tensor_tensor(top_p[:, :, :], top_e[:, :, :],
                                               inv[:, :].unsqueeze(2).to_broadcast([P, NT, TOPK]), ALU.mult))
            chain.link(nc.vector.tensor_reduce(total[:, :], top_p[:, :, :], AXX, ALU.add))
            chain.link(nc.vector.tensor_scalar(total[:, :], total[:, :], 1e-20, None, ALU.add))
            chain.link(nc.vector.reciprocal(inv[:, :], total[:, :]))
            chain.link(nc.vector.tensor_tensor(weights[:, :, :], top_p[:, :, :],
                                               inv[:, :].unsqueeze(2).to_broadcast([P, NT, TOPK]), ALU.mult))
            chain.link(nc.vector.tensor_copy(top_f[:, :, :], top_i[:, :, 0:TOPK]))
            v.wait_ge(got, 16 * len(loads))
            for j in range(TOPK):
                last = nc.vector.tensor_tensor(hot[:, j, :, :], iota_e[:, :].unsqueeze(1).to_broadcast([P, NT, NE]),
                                               top_f[:, :, j:j + 1].to_broadcast([P, NT, NE]), ALU.is_equal)
            chain.link(last)
            chain.link(nc.vector.tensor_tensor(mask[:, :, :], hot[:, 0, :, :], hot[:, 1, :, :], ALU.add))
            chain.link(nc.vector.tensor_tensor(mask[:, :, :], mask[:, :, :], hot[:, 2, :, :], ALU.add))
            v.sem_inc(mask_made, 1)
            v.wait_ge(counted, 1)
            chain.link(nc.vector.tensor_copy(tile_sum[:, :, :], ps_total[:, :, :].rearrange("p t e -> p e t")))
            chain.link(nc.vector.tensor_tensor_scan(
                running[:, :, :].rearrange("p e t -> p (e t)"), not_first[:, :, :].rearrange("p e t -> p (e t)"),
                tile_sum[:, :, :].rearrange("p e t -> p (e t)"), 0.0, ALU.mult, ALU.add))
            chain.link(nc.vector.tensor_tensor(excl[:, :, :], running[:, :, :], tile_sum[:, :, :], ALU.subtract))
            chain.link(nc.vector.tensor_tensor(
                filled[:, :, :], running[:, :, NT - 1:NT].to_broadcast([P, NE, NT]),
                iota_m[:, :].unsqueeze(1).to_broadcast([P, NE, NT]), ALU.is_gt))
            chain.link(nc.vector.tensor_reduce(n_tiles[:, :], filled[:, :, :], AXX, ALU.add))
            chain.link(nc.vector.tensor_tensor_scan(tile_end[:, :], ones[:, 0:NE], n_tiles[:, :], 0.0,
                                                    ALU.mult, ALU.add))
            chain.link(nc.vector.tensor_tensor(base[:, :], tile_end[:, :], n_tiles[:, :], ALU.subtract))
            chain.link(nc.vector.scalar_tensor_tensor(
                excl[:, :, :], base[:, :].unsqueeze(2).to_broadcast([P, NE, NT]), float(P), excl[:, :, :],
                ALU.mult, ALU.add))
            chain.link(nc.vector.tensor_tensor(slot[:, :, :], excl[:, :, :].rearrange("p e t -> p t e"),
                                               ps_before[:, :, :], ALU.add))
            for j in range(TOPK):
                chain.link(nc.vector.tensor_tensor(picked[:, :, :], slot[:, :, :], hot[:, j, :, :], ALU.mult))
                last = nc.vector.tensor_reduce(slot_f[:, j, :], picked[:, :, :], AXX, ALU.add)
                if j < TOPK - 1:
                    chain.link(last)
            last.then_inc(own, 1)
            v.wait_ge(own, 1)
            chain.link(nc.vector.tensor_copy(slot_of[:, :, :], slot_f[:, :, :]))
            chain.close()
            nc.vector.tensor_tensor(past[:, :, :], iota_s[:, :].unsqueeze(2).to_broadcast([1, SLOT_TILES, NE]),
                                    tile_end[0:1, :].unsqueeze(1).to_broadcast([1, SLOT_TILES, NE]),
                                    ALU.is_ge).then_inc(own, 1)
            v.wait_ge(own, 2)
            nc.vector.tensor_reduce(exp_f[:, :], past[:, :, :], AXX, ALU.add).then_inc(own, 1)
            v.wait_ge(own, 3)
            nc.vector.tensor_scalar(expert_of[:, :], exp_f[:, :], float(NE - 1), None, ALU.min).then_inc(own, 1)
            v.wait_ge(own, 4)


class SharedExpert:

    def __init__(self, nc, ctx, X, ident, ffn, tag, signals):
        def sb(name, shape, dt=F32):
            return ctx.enter_context(nc.sbuf_tensor(tag + name, shape, dt))

        def ps(name, shape, dt=F32):
            return ctx.enter_context(nc.psum_tensor(tag + name, shape, dt))

        self.nc, self.X, self.ident, self.ffn = nc, X, ident, ffn
        self.x = sb("x", [P, TT, D])
        self.xT = [sb(f"xT{j}", [P, DC, L]) for j in range(2)]
        self.gate = sb("gate", [P, FSC, L])
        self.act_T = sb("act", [P, FSC, L])
        self.y = sb("y", [P, TT, D])
        self.ps_x = ps("ps_x", [P, DC, L])
        self.ps_u = ps("ps_u", [P, FSC, L])
        self.ps_g = ps("ps_g", [P, FSC, L])
        self.ps_y = ps("ps_y", [P, TT, D])
        (self.copied, self.turned, self.xT_made, self.up_done, self.gate_done, self.gelu_made, self.acted,
         self.down_done, self.y_made, self.x_made) = signals

    @staticmethod
    def signals(nc, ctx):
        return [ctx.enter_context(nc.semaphore("s_" + n)) for n in (
            "copied", "turned", "xT_made", "up_done", "gate_done", "gelu_made", "acted",
            "down_done", "y_made", "x_made")]

    def copy_x(self, act, b):
        at = bass.ds(b * TT, TT)
        self.nc.scalar.activation(self.x[:, :, :], self.X[:, at, :], ACT.Copy).then_inc(self.copied, 1)

    def take_xT(self, act, b, q):
        act.wait_ge(self.turned, b + 1)
        self.nc.scalar.activation(self.xT[q][:, :, :], self.ps_x[:, :, :], ACT.Copy).then_inc(self.xT_made, 1)

    def gelu(self, act, b):
        act.wait_ge(self.gate_done, b + 1)
        act.wait_ge(self.acted, b + 1)
        for c in range(FSC):
            last = self.nc.scalar.activation(self.gate[:, c, :], self.ps_g[:, c, :], ACT.Gelu,
                                             bias=self.ffn.b_up[:, FSC + c:FSC + c + 1])
        last.then_inc(self.gelu_made, 1)

    def act_start(self, act, b):
        act.preload_act_table_set("gelu_and_others")
        self.copy_x(act, b)
        self.take_xT(act, b, 0)

    def act_step(self, act, b, q, more):
        if more:
            self.copy_x(act, b + 1)
        self.gelu(act, b)
        if more:
            self.take_xT(act, b + 1, 1 - q)

    def gated_units(self, v, b):
        nc = self.nc
        v.wait_ge(self.gelu_made, b + 1)
        v.wait_ge(self.up_done, b + 1)
        for c in range(FSC):
            last = nc.vector.scalar_tensor_tensor(self.act_T[:, c, :], self.ps_u[:, c, :],
                                                  self.ffn.b_up[:, c:c + 1], self.gate[:, c, :],
                                                  ALU.add, ALU.mult)
        last.then_inc(self.acted, 1)

    def add_to_x(self, v, b, rows_sent=None):
        nc, at = self.nc, bass.ds(b * TT, TT)
        v.wait_ge(self.down_done, b + 1)
        nc.vector.tensor_tensor(self.y[:, :, :], self.ps_y[:, :, :],
                                self.ffn.b_down[:, :].unsqueeze(1).to_broadcast([P, TT, D]),
                                ALU.add).then_inc(self.y_made, 1)
        if rows_sent is not None:
            v.wait_ge(rows_sent, b + 1)
        v.wait_ge(self.y_made, b + 1)
        nc.vector.tensor_tensor(self.X[:, at, :], self.y[:, :, :], self.X[:, at, :],
                                ALU.add).then_inc(self.x_made, 1)
        v.wait_ge(self.x_made, b + 1)

    def transposes(self, pe, b):
        pe.wait_ge(self.copied, b + 1)
        for c in range(DC):
            for s in range(TT):
                last = self.nc.tensor.transpose(self.ps_x[:, c, s * P:(s + 1) * P],
                                                self.x[:, s, c * P:(c + 1) * P], self.ident[:, :])
        last.then_inc(self.turned, 1)

    def up(self, pe, dst, q, at, done):
        for c in range(FSC):
            for k in range(DC):
                last = self.nc.tensor.matmul(dst[:, c, :], self.ffn.up[:, k, at + c * P:at + (c + 1) * P],
                                             self.xT[q][:, k, :], start=(k == 0), stop=(k == DC - 1))
        last.then_inc(done, 1)

    def tensor_start(self, pe, b):
        if b == 0:
            pe.sem_inc(self.acted, 1)
        self.transposes(pe, b)
        pe.wait_ge(self.xT_made, b + 1)
        self.up(pe, self.ps_g, 0, FS, self.gate_done)

    def tensor_step(self, pe, b, q, more, first=False):
        pe.wait_ge(self.acted, b + 1)
        self.up(pe, self.ps_u, q, 0, self.up_done)
        if more:
            self.transposes(pe, b + 1)
            pe.wait_ge(self.xT_made, b + 2)
            pe.wait_ge(self.gelu_made, b + 1)
            self.up(pe, self.ps_g, 1 - q, FS, self.gate_done)
        pe.wait_ge(self.acted, b + 2)
        if not first:
            pe.wait_ge(self.y_made, b)
        for s in range(TT):
            for k in range(FSC):
                last = self.nc.tensor.matmul(self.ps_y[:, s, :], self.act_T[:, k, s * P:(s + 1) * P],
                                             self.ffn.down[:, k, :], start=(k == 0), stop=(k == FSC - 1))
        last.then_inc(self.down_done, 1)


def scatter_phase(nc, dram, X, ident, ffn, signals, w1, slot_of, slots_dram):
    with ExitStack() as ctx:
        half = B // 2
        shared = SharedExpert(nc, ctx, X, ident, ffn, "c_", signals)
        sent = [ctx.enter_context(nc.semaphore(f"c_sent{j}")) for j in range(2)]
        rows_sent = ctx.enter_context(nc.semaphore("c_rows_sent"))
        w_in = ctx.enter_context(nc.semaphore("c_w_in"))
        block = ctx.enter_context(nc.Block())

        def steps(eng, body):
            body(0, 0, True)
            with eng.Fori(0, half // 2 - 1) as i:
                body(i * 2 + 1, 1, True)
                body(i * 2 + 2, 0, True)
            body(half - 1, 1, False)

        @block.sync
        def _(sp):
            w1_v = dram["fc1T"].rearrange("e (c p) f -> p e c f", p=P)
            for e in range(NE):
                sp.dma_start(w1[:, e, :, :], w1_v[:, e, :, :]).then_inc(w_in, 16)
            sp.wait_ge(w_in, 16 * NE)

        @block.gpsimd
        def _(g):
            for b in range(B):
                for t in range(b * TT, (b + 1) * TT):
                    for j in range(TOPK):
                        g.indirect_dma_start(
                            out=slots_dram, out_offset=bass.IndirectOffsetOnAxis(ap=slot_of[:, j, t:t + 1], axis=0),
                            in_=X[:, t, :], in_offset=None).then_inc(sent[b % 2], 16)
                if b > 0:
                    g.wait_ge(sent[(b - 1) % 2], 16 * TT * TOPK * ((b - 1) // 2 + 1))
                    g.sem_inc(rows_sent, 1)
            g.wait_ge(sent[(B - 1) % 2], 16 * TT * TOPK * (B // 2))

        @block.scalar
        def _(act):
            shared.act_start(act, 0)
            steps(act, lambda b, q, more: shared.act_step(act, b, q, more))

        @block.vector
        def _(v):
            def step(b, q, more):
                shared.gated_units(v, b)
                shared.add_to_x(v, b, rows_sent)

            steps(v, step)

        @block.tensor
        def _(pe):
            shared.tensor_start(pe, 0)
            steps(pe, lambda b, q, more: shared.tensor_step(pe, b, q, more, isinstance(b, int) and b == 0))


def expert_phase(nc, ident, ffn, w1, expert_of, slots_dram, y_dram):
    with ExitStack() as ctx:
        def sb(name, shape, dt=F32):
            return ctx.enter_context(nc.sbuf_tensor(name, shape, dt))

        def ps(name, shape, dt=F32):
            return ctx.enter_context(nc.psum_tensor(name, shape, dt))

        def sem(name):
            return ctx.enter_context(nc.semaphore(name))

        FC = FEC
        R = 4
        w2, rows = ffn.e_down, ffn.rows
        ones = sb("eones", [PARTS, P], BF16)
        xg = [sb(f"xg{j}", [P, D]) for j in range(R)]
        xT = [sb(f"e_xT{j}", [P, DC, P]) for j in range(2)]
        gate = [sb(f"e_gate{j}", [P, FE]) for j in range(2)]
        act_s = [sb(f"e_act{j}", [P, FE]) for j in range(2)]
        aT = [sb(f"e_aT{j}", [P, FC, P]) for j in range(2)]
        y = [sb(f"e_y{j}", [P, D]) for j in range(R)]
        ps_x = [ps(f"e_ps_x{j}", [P, DC, P]) for j in range(2)]
        ps_h = [ps(f"e_ps_h{j}", [P, 2 * FE]) for j in range(2)]
        ps_a = [ps(f"e_ps_a{j}", [P, FC, P]) for j in range(2)]
        ps_y = [ps(f"e_ps_y{j}", [P, D]) for j in range(2)]
        ones_made = sem("e_ones_made")
        x_in = [sem(f"e_x_in{j}") for j in range(R)]
        y_out = [sem(f"e_y_out{j}") for j in range(R)]
        e_tr, e_xT, e_h, e_gate, e_act, e_ta, e_aT, e_yp, e_y = (
            sem("e_" + n) for n in ("tr", "xT", "h", "gate", "act", "ta", "aT", "yp", "y"))
        block = ctx.enter_context(nc.Block())
        ROUNDS = SLOT_TILES // R

        def steps(eng, body):
            with eng.Fori(0, ROUNDS - 1) as i:
                for j in range(R):
                    body(i, j, False)
            for j in range(R):
                body(ROUNDS - 1, j, True)

        @block.sync
        def _(sp):
            for j in range(R):
                sp.dma_start(xg[j][:, :], slots_dram[j * P:(j + 1) * P, :]).then_inc(x_in[j], 16)

            slot_v = slots_dram.rearrange("(i p) d -> p i d", p=P)
            y_v = y_dram.rearrange("(i p) d -> p i d", p=P)

            def step(i, j, last):
                t = i * R + j
                sp.wait_ge(e_y, t + 1)
                sp.dma_start(y_v[:, bass.ds(t, 1), :], y[j][:, :].unsqueeze(1)).then_inc(y_out[j], 16)
                if not last:
                    sp.dma_start(xg[j][:, :].unsqueeze(1), slot_v[:, bass.ds(t + R, 1), :]).then_inc(x_in[j], 16)

            steps(sp, step)
            for j in range(R):
                sp.wait_ge(y_out[j], 16 * ROUNDS + 16)

        @block.gpsimd
        def _(g):
            nc.gpsimd.memset(ones[:, :], 1.0).then_inc(ones_made, 1)

        @block.scalar
        def _(act):
            act.preload_act_table_set("gelu_and_others")
            for j in range(R):
                act.sem_inc(y_out[j], 16)

            def take_x(t, j):
                act.wait_ge(e_tr, t + 1)
                nc.scalar.activation(xT[j % 2][:, :, :], ps_x[j % 2][:, :, :], ACT.Copy).then_inc(e_xT, 1)

            def gelu(t, j):
                act.wait_ge(e_h, t + 1)
                nc.scalar.activation(gate[j % 2][:, :], ps_h[j % 2][:, FE:], ACT.Gelu).then_inc(e_gate, 1)

            def step(i, j, last):
                t = i * R + j
                if not last or j < R - 2:
                    take_x(t + 2, j)
                if not last or j < R - 1:
                    gelu(t + 1, j + 1)
                act.wait_ge(e_yp, t + 1)
                act.wait_ge(y_out[j], i * 16 + 16)
                nc.scalar.activation(y[j][:, :], ps_y[j % 2][:, :], ACT.Copy).then_inc(e_y, 1)

            take_x(0, 0)
            take_x(1, 1)
            gelu(0, 0)
            steps(act, step)

        @block.vector
        def _(v):
            def multiply(t, j):
                v.wait_ge(e_gate, t + 1)
                nc.vector.tensor_tensor(act_s[j % 2][:, :], ps_h[j % 2][:, 0:FE], gate[j % 2][:, :],
                                        ALU.mult).then_inc(e_act, 1)

            def step(i, j, last):
                t = i * R + j
                v.wait_ge(e_ta, t + 1)
                nc.vector.tensor_copy(aT[j % 2][:, :, :], ps_a[j % 2][:, :, :]).then_inc(e_aT, 1)
                if not last or j < R - 1:
                    multiply(t + 1, j + 1)

            multiply(0, 0)
            steps(v, step)

        @block.tensor
        def _(pe):
            pe.wait_ge(ones_made, 1)

            def turn_x(t, round_, j):
                pe.wait_ge(x_in[j], round_ * 16 + 16)
                for c in range(DC):
                    last = nc.tensor.transpose(ps_x[j % 2][:, c, :], xg[j][:, c * P:(c + 1) * P], ident[:, :])
                last.then_inc(e_tr, 1)

            def expert(t):
                return pe.value_load(expert_of[0:1, bass.ds(t, 1)], min_val=0, max_val=NE - 1)

            def up(t, j, e):
                pe.wait_ge(e_xT, t + 1)
                nc.tensor.matmul(ps_h[j % 2][:, :], ones[:, :], rows[:, bass.ds(e, 1), 0:2 * FE],
                                 start=True, stop=False)
                for k in range(DC):
                    last = nc.tensor.matmul(ps_h[j % 2][:, :], xT[j % 2][:, k, :], w1[:, bass.ds(e, 1), k, :],
                                            start=False, stop=(k == DC - 1))
                last.then_inc(e_h, 1)

            def step(i, j, last):
                t = i * R + j
                e = expert(t)
                if not last or j < R - 1:
                    e_next = expert(t + 1)
                if not last or j < R - 2:
                    turn_x(t + 2, i + (j + 2) // R, (j + 2) % R)
                pe.wait_ge(e_act, t + 1)
                for c in range(FC):
                    done = nc.tensor.transpose(ps_a[j % 2][:, c, :], act_s[j % 2][:, c * P:(c + 1) * P], ident[:, :])
                done.then_inc(e_ta, 1)
                if not last or j < R - 1:
                    up(t + 1, (j + 1) % R, e_next)
                pe.wait_ge(e_aT, t + 1)
                nc.tensor.matmul(ps_y[j % 2][:, :], ones[:, :], rows[:, bass.ds(e, 1), 2 * FE:],
                                 start=True, stop=False)
                for k in range(FC):
                    done = nc.tensor.matmul(ps_y[j % 2][:, :], aT[j % 2][:, k, :], w2[:, bass.ds(e, 1), k, :],
                                            start=False, stop=(k == FC - 1))
                done.then_inc(e_yp, 1)

            turn_x(0, 0, 0)
            turn_x(1, 0, 1)
            up(0, 0, expert(0))
            steps(pe, step)


def combine_phase(nc, X, ident, ffn, signals, weights, slot_of, y_dram, out):
    with ExitStack() as ctx:
        def sb(name, shape, dt=F32):
            return ctx.enter_context(nc.sbuf_tensor(name, shape, dt))

        def sem(name):
            return ctx.enter_context(nc.semaphore(name))

        half = B // 2
        shared = SharedExpert(nc, ctx, X, ident, ffn, "d_", signals)
        R = 8
        PER = NT // half
        rows = sb("e_rows_in", [P, R, TOPK, D])
        stats, mv = sb("d_stats", [P, NT, 6]), sb("d_mv", [P, NT, 2])
        var, root, r0, r1, r2 = (sb("d_" + n, [P, NT]) for n in ("var", "root", "r0", "r1", "r2"))
        got = [sem(f"d_got{r}") for r in range(R)]
        used, chain_s, var_made, root_made, normed, stored, settled = (
            sem("d_" + n) for n in ("used", "chain", "var", "root", "normed", "stored", "settled"))
        block = ctx.enter_context(nc.Block())
        ENDS = (3, 6, 7)
        groups = [(0 if i == 0 else (ENDS[i - 1] + 1) * PER, (end + 1) * PER) for i, end in enumerate(ENDS)]

        @block.gpsimd
        def _(g):
            for t in range(NT):
                if t >= R:
                    g.wait_ge(used, t - R + 1)
                for j in range(TOPK):
                    g.indirect_dma_start(
                        out=rows[:, t % R, j, :], out_offset=None, in_=y_dram,
                        in_offset=bass.IndirectOffsetOnAxis(ap=slot_of[:, j, t:t + 1], axis=0)).then_inc(
                            got[t % R], 16)

        @block.scalar
        def _(act):
            def take_root(i):
                a, z = groups[i]
                act.preload_act_table_set("sqrt_and_others")
                act.wait_ge(var_made, i + 1)
                nc.scalar.activation(root[:, a:z], var[:, a:z], ACT.Sqrt).then_inc(root_made, 1)
                if i < len(groups) - 1:
                    act.preload_act_table_set("gelu_and_others")

            shared.act_start(act, half)
            for r in range(half):
                shared.act_step(act, half + r, r % 2, r < half - 1)
                if r in ENDS:
                    take_root(ENDS.index(r))

        @block.vector
        def _(v):
            chain = Chain(v, chain_s, 0, TOPK * NT + 7 * len(groups))

            def combine(t):
                v.wait_ge(got[t % R], 16 * TOPK * (t // R + 1))
                for j in range(TOPK):
                    chain.link(nc.vector.scalar_tensor_tensor(
                        X[:, t, :], rows[:, t % R, j, :], weights[:, t, j:j + 1], X[:, t, :],
                        ALU.mult, ALU.add))
                v.sem_inc(used, 1)
                nc.vector.bn_stats(stats[:, t, :], X[:, t, :]).then_inc(settled, 1)

            def normalise(i):
                a, z = groups[i]
                v.wait_ge(settled, z)
                for t in range(a, z):
                    last = nc.vector.bn_aggr(mv[:, t, :], stats[:, t, :])
                chain.link(last)
                chain.link(nc.vector.tensor_scalar(var[:, a:z], mv[:, a:z, 1], EPS, None, ALU.add))
                v.sem_inc(var_made, 1)
                v.wait_ge(root_made, i + 1)
                chain.link(nc.vector.reciprocal(r0[:, a:z], root[:, a:z]))
                chain.link(nc.vector.tensor_tensor(r1[:, a:z], r0[:, a:z], r0[:, a:z], ALU.mult))
                chain.link(nc.vector.tensor_tensor(r1[:, a:z], r1[:, a:z], var[:, a:z], ALU.mult))
                chain.link(nc.vector.tensor_scalar(r1[:, a:z], r1[:, a:z], -0.5, 1.5, ALU.mult, ALU.add))
                chain.link(nc.vector.tensor_tensor(r2[:, a:z], r1[:, a:z], r0[:, a:z], ALU.mult))
                for t in range(a, z):
                    nc.vector.tensor_scalar(X[:, t, :], X[:, t, :], mv[:, t, 0:1], r2[:, t:t + 1],
                                            ALU.subtract, ALU.mult).then_inc(normed, 1)

            for r in range(half):
                shared.gated_units(v, half + r)
                for t in range(r * PER, r * PER + PER // 2):
                    combine(t)
                shared.add_to_x(v, half + r)
                for t in range(r * PER + PER // 2, (r + 1) * PER):
                    combine(t)
                if r in ENDS:
                    normalise(ENDS.index(r))
            chain.close()

        @block.tensor
        def _(pe):
            shared.tensor_start(pe, half)
            for r in range(half):
                shared.tensor_step(pe, half + r, r % 2, r < half - 1)

        @block.sync
        def _(sp):
            o = out.rearrange("b (s p) d -> p (b s) d", p=P)
            for a, z in groups:
                sp.wait_ge(normed, z)
                sp.dma_start(o[:, a:z, :], X[:, a:z, :]).then_inc(stored, 16)
            sp.wait_ge(stored, 16 * len(groups))


def load_consts(nc, dram, ident):
    with nc.semaphore("ident_in") as got, nc.Block() as block:
        @block.sync
        def _(sp):
            sp.dma_start(ident[:, :], dram["ident"]).then_inc(got, 16)
            sp.wait_ge(got, 16)


def build(nc, dram, out):
    slots_dram = nc.dram_tensor("slot_rows", (SLOT_TILES * P, D), F32, kind="Internal").ap()
    y_dram = nc.dram_tensor("slot_results", (SLOT_TILES * P, D), F32, kind="Internal").ap()
    with ExitStack() as ctx:
        def sb(name, shape, dt=F32):
            return ctx.enter_context(nc.sbuf_tensor(name, shape, dt))

        ident = sb("ident", [P, P])
        X = sb("X", [P, NT, D])
        weights = sb("weights", [P, NT, TOPK])
        slot_of = sb("slot_of", [P, TOPK, NT], mybir.dt.uint32)
        expert_of = sb("expert_of", [1, SLOT_TILES], mybir.dt.int32)
        load_consts(nc, dram, ident)
        mamba_phase(nc, dram, X, ident)
        ffn = FfnWeights(nc, ctx)
        with nc.sbuf_tensor("logits", [P, NT, 16], F32) as logits:
            attention_phase(nc, dram, X, ident, ffn, logits, slots_dram)
            route_phase(nc, dram, logits, weights, slot_of, expert_of)
        signals = SharedExpert.signals(nc, ctx)
        with nc.sbuf_tensor("w1", [P, NE, DC, 2 * FE], F32) as w1:
            scatter_phase(nc, dram, X, ident, ffn, signals, w1, slot_of, slots_dram)
            expert_phase(nc, ident, ffn, w1, expert_of, slots_dram, y_dram)
        combine_phase(nc, X, ident, ffn, signals, weights, slot_of, y_dram, out)


def kernel(**inputs):
    import numpy as _np
    import concourse.bacc as _bacc
    from concourse import mybir as _mybir
    from concourse.bass_utils import run_bass_kernel_spmd as _run

    i = {k: _np.asarray(a) for k, a in inputs.items()}

    def col(a):
        return a.reshape(-1, P, *a.shape[1:]).swapaxes(0, 1)

    def pad_heads(a):
        return _np.concatenate([a.reshape(NH, DK, D), _np.zeros((NH, 32 - DK, D), a.dtype)], 1).reshape(-1, D)

    theta = _np.float32(10000.0) ** (_np.float32(-2.0) * _np.arange(D // 2, dtype=_np.float32) / _np.float32(D))
    angle = _np.arange(1, L + 1, dtype=_np.float32)[:, None] * theta
    cos, sin = (_np.repeat(f(angle), 2, axis=-1).astype(_np.float32) for f in (_np.cos, _np.sin))
    arrays = {
        "x": i["x"], "norm_w": col(i["L0_attn_norm_w"]),
        "in_wT": i["L0_attn_in_w"].T, "skip_wT": i["L0_attn_skip_w"].T,
        "conv_w": col(i["L0_attn_conv_w"][:, 0, :]), "conv_b": col(i["L0_attn_conv_b"]),
        "dbc_wT": _np.concatenate([i["L0_attn_Wd1"]] + [i["L0_attn_WB"], i["L0_attn_WC"]] * PARTS).T,
        "Wd2T": i["L0_attn_Wd2_w"].T, "Wd2_b": col(i["L0_attn_Wd2_b"]),
        "A_log": col(i["L0_attn_A_log"]), "W_D": col(i["L0_attn_W_D"]), "out_wT": i["L0_attn_out_w"].T,
        "pick": _np.tile(_np.eye(NBC, dtype=_np.float32), (PARTS, 1)),
        "ident": _np.eye(P, dtype=_np.float32),
        "s_fc1T": i["L0_ffn_s_fc1_w"].T, "s_fc2T": i["L0_ffn_s_fc2_w"].T,
        "s_fc1_b": col(i["L0_ffn_s_fc1_b"]), "s_mult": col(i["L0_ffn_s_geglu_mult"]),
        "s_fc2_b": i["L0_ffn_s_fc2_b"][None], "gateT": i["L0_ffn_gate_w"].T,
        "fc1T": i["L0_ffn_fc1_w"].swapaxes(1, 2), "fc2T": i["L0_ffn_fc2_w"].swapaxes(1, 2),
        "e_bias": _np.concatenate([i["L0_ffn_fc1_b"], i["L0_ffn_fc2_b"]], 1).reshape(P, -1),
        "e_mult": i["L0_ffn_geglu_mult"].reshape(NE, FE // P, P).transpose(2, 0, 1),
        "tri": _np.triu(_np.ones((P, P), _np.float32), 1), "ones": _np.ones((P, P), _np.float32),
        "iota": _np.arange(P, dtype=_np.float32)[None], "iota_m": _np.arange(NT, dtype=_np.float32)[None] * P,
        "not_first": _np.tile((_np.arange(NT) > 0).astype(_np.float32), NE)[None],
        "ctxT": i["ctx_1024"].transpose(0, 2, 1),
        "WqT": i["L0_xattn_Wq_w"].T, "WkT": i["L0_xattn_Wk_w"].T, "WvT": i["L0_xattn_Wv_w"].T,
        "WoT": pad_heads(i["L0_xattn_Wo_w"].T),
        "bq": col(i["L0_xattn_Wq_b"]), "bk": col(i["L0_xattn_Wk_b"]),
        "bv": i["L0_xattn_Wv_b"][None], "bo": i["L0_xattn_Wo_b"][None],
        "head_rows": _np.repeat(_np.eye(HC, dtype=_np.float32), DK, axis=0),
        "cosT": cos.T, "sinT": _np.concatenate([-sin.T[:D // 2], sin.T[D // 2:]]),
    }
    arrays = {k: _np.ascontiguousarray(a) for k, a in arrays.items()}
    nc = _bacc.Bacc("TRN2", target_bir_lowering=False, num_devices=1)
    dram = {k: nc.dram_tensor(f"in_{k}", a.shape, _mybir.dt.from_np(a.dtype), kind="ExternalInput").ap()
            for k, a in arrays.items()}
    out = nc.dram_tensor("out_0", (B, L, D), _mybir.dt.float32, kind="ExternalOutput").ap()
    build(nc, dram, out)
    r = _run(nc, [{f"in_{k}": a for k, a in arrays.items()}], core_ids=[0])
    return r.results[0]["out_0"]
```
